# Optimizing a Trainium2 kernel written in Bass

```python
import numpy as np
import jax
import jax.numpy as jnp

def _softmax(x, axis=-1):
    return jax.nn.softmax(x, axis=axis)

def _gelu(x):
    return jax.nn.gelu(x, approximate=True)

def _silu(x):
    return jax.nn.silu(x)

def _sigmoid(x):
    return jax.nn.sigmoid(x)

def _layernorm(x, axis=-1, eps=1e-05):
    m = jnp.mean(x, axis=axis, keepdims=True)
    v = jnp.var(x, axis=axis, keepdims=True)
    return (x - m) / jnp.sqrt(v + eps)

def _scatter_add(tgt, idx, src, axis=0):
    return tgt.at[idx].add(src)

def _segment_sum(src, seg, n):
    return jax.ops.segment_sum(src, seg, n)
kernel_name = 'mk_xattn_ffn_d1_seqx_r8_e82345'

def setup_inputs(seed: int=0):
    np.random.seed(seed)
    _w = jnp.asarray

    def _rec_inputs():
        import jax
        import jax.numpy as jnp
        _rk = jax.random.key(seed)
        x = -0.0002928 + 1 * jax.random.normal(jax.random.fold_in(_rk, 1), (32, 128, 128), jnp.float32)
        _lenS = 128 - jax.random.randint(jax.random.fold_in(_rk, 7), (32,), 0, max(1, 128 // 4) + 1, jnp.int32)
        _lenS2 = 128 - jax.random.randint(jax.random.fold_in(_rk, 8), (32,), 0, max(1, 128 // 4) + 1, jnp.int32)
        _ctx_1024P = jax.random.normal(jax.random.fold_in(_rk, 11), (32, 16, 128), jnp.float32)
        _ctx_1024c = jax.random.dirichlet(jax.random.fold_in(_rk, 511), 0.3 * jnp.ones((16,), jnp.float32), (32, 128))
        _ctx_1024t = jnp.einsum('bsk,bkd->bsd', _ctx_1024c, _ctx_1024P)
        _ctx_1024t = _ctx_1024t * jax.lax.rsqrt(jnp.mean(jnp.square(_ctx_1024t)) + 1e-12) * 0.953939
        ctx_1024 = 2.81802e-05 + 1.00001 * (_ctx_1024t + 0.3 * jax.random.normal(jax.random.fold_in(_rk, 611), (32, 128, 128), jnp.float32))
        _validS = jnp.arange(128)[None, :] < _lenS[:, None]
        _validS2 = jnp.arange(128)[None, :] < _lenS2[:, None]
        _causal = jnp.tril(jnp.ones((128, 128), dtype=bool))
        mask_BxS2_bk0 = jnp.logical_not(jnp.broadcast_to(_validS2[:, :], (32, 128)))
        return (x, ctx_1024, mask_BxS2_bk0)
    x, ctx_1024, mask_BxS2_bk0 = _rec_inputs()

    def _L0_xattn_setup():
        import jax, jax.numpy as jnp
        import numpy as np
        NUM_HEADS, NUM_KV, HEAD_DIM, WIDTH = (4, 1, 32, 128)
        MASK_FILL = -2.3819763e+38

        def _apply_rope(x, positions, max_wavelength=10000.0):
            d = x.shape[-1]
            freq_exp = 2.0 / d * jnp.arange(d // 2, dtype=jnp.float32)
            timescale = max_wavelength ** freq_exp
            radians = positions[..., None].astype(jnp.float32) / timescale
            radians = radians[..., None, :]
            sin, cos = (jnp.sin(radians), jnp.cos(radians))
            x1, x2 = jnp.split(x, 2, axis=-1)
            out = jnp.concatenate([x1 * cos - x2 * sin, x2 * cos + x1 * sin], axis=-1)
            return out.astype(x.dtype)

        def _rmsnorm(x, scale):
            var = jnp.mean(jnp.square(x.astype(jnp.float32)), axis=-1, keepdims=True)
            normed = x * jax.lax.rsqrt(var + 1e-06)
            return (normed * (1 + scale)).astype(x.dtype)
        key = jax.random.key(seed)
        ks = jax.random.split(key, 7)
        B, T, S = (8, 64, 256)
        return {'x': jax.random.normal(ks[0], (B, T, WIDTH), jnp.float32), 'mem_seq': jax.random.normal(ks[1], (B, S, WIDTH), jnp.float32), 'mem_mask': jax.random.randint(ks[2], (B, S), 0, 2).astype(bool), 'rms_scale': jax.random.normal(ks[3], (WIDTH,), jnp.float32) * 0.02, 'q_w': jax.random.normal(ks[4], (NUM_HEADS, WIDTH, HEAD_DIM), jnp.float32) / np.sqrt(WIDTH), 'kv_w': jax.random.normal(ks[5], (2, NUM_KV, WIDTH, HEAD_DIM), jnp.float32) / np.sqrt(WIDTH), 'out_w': jax.random.normal(ks[6], (NUM_HEADS, HEAD_DIM, WIDTH), jnp.float32) / np.sqrt(NUM_HEADS * HEAD_DIM)}
    _L0_xattn_all = _L0_xattn_setup()
    _L0_xattn_in = {k: v for k, v in _L0_xattn_all.items() if k in ('rms_scale', 'q_w', 'kv_w', 'out_w')}
    del _L0_xattn_all

    def _L0_ffn_setup():
        import jax, jax.numpy as jnp
        import numpy as np
        S, B, D, H, E, K, F = (128, 4, 128, 16, 8, 2, 512)

        def _ln(x, g, b, eps=1e-05):
            mu = jnp.mean(x, axis=-1, keepdims=True)
            var = jnp.mean((x - mu) ** 2, axis=-1, keepdims=True)
            return (x - mu) * jax.lax.rsqrt(var + eps) * g + b
        key = jax.random.key(seed)
        ks = jax.random.split(key, 8)
        s = 0.02
        return {'src': jax.random.normal(ks[0], (S, B, D), jnp.float32), 'in_proj_w': jax.random.normal(ks[1], (3 * D, D), jnp.float32) * s, 'in_proj_b': jnp.zeros((3 * D,), jnp.float32), 'out_w': jax.random.normal(ks[2], (D, D), jnp.float32) * s, 'out_b': jnp.zeros((D,), jnp.float32), 'gate_w': jax.random.normal(ks[3], (E, D), jnp.float32) * s, 'gate_b': jnp.zeros((E,), jnp.float32), 'w1': jax.random.normal(ks[4], (E, F, D), jnp.float32) * s, 'b1': jnp.zeros((E, F), jnp.float32), 'w2': jax.random.normal(ks[5], (E, D, F), jnp.float32) * s, 'b2': jnp.zeros((E, D), jnp.float32), 'ln1_g': jnp.ones((D,), jnp.float32), 'ln1_b': jnp.zeros((D,), jnp.float32), 'ln2_g': jnp.ones((D,), jnp.float32), 'ln2_b': jnp.zeros((D,), jnp.float32)}
    _L0_ffn_all = _L0_ffn_setup()
    _L0_ffn_in = {k: v for k, v in _L0_ffn_all.items() if k in ('in_proj_w', 'in_proj_b', 'out_w', 'out_b', 'gate_w', 'gate_b', 'w1', 'b1', 'w2', 'b2', 'ln1_g', 'ln1_b', 'ln2_g', 'ln2_b')}
    del _L0_ffn_all
    return {'x': x, 'ctx_1024': ctx_1024, 'mask_BxS2_bk0': mask_BxS2_bk0, 'L0_xattn_rms_scale': _L0_xattn_in['rms_scale'], 'L0_xattn_q_w': _L0_xattn_in['q_w'], 'L0_xattn_kv_w': _L0_xattn_in['kv_w'], 'L0_xattn_out_w': _L0_xattn_in['out_w'], 'L0_ffn_in_proj_w': _L0_ffn_in['in_proj_w'], 'L0_ffn_in_proj_b': _L0_ffn_in['in_proj_b'], 'L0_ffn_out_w': _L0_ffn_in['out_w'], 'L0_ffn_out_b': _L0_ffn_in['out_b'], 'L0_ffn_gate_w': _L0_ffn_in['gate_w'], 'L0_ffn_gate_b': _L0_ffn_in['gate_b'], 'L0_ffn_w1': _L0_ffn_in['w1'], 'L0_ffn_b1': _L0_ffn_in['b1'], 'L0_ffn_w2': _L0_ffn_in['w2'], 'L0_ffn_b2': _L0_ffn_in['b2'], 'L0_ffn_ln1_g': _L0_ffn_in['ln1_g'], 'L0_ffn_ln1_b': _L0_ffn_in['ln1_b'], 'L0_ffn_ln2_g': _L0_ffn_in['ln2_g'], 'L0_ffn_ln2_b': _L0_ffn_in['ln2_b']}

def reference(x, ctx_1024, mask_BxS2_bk0, L0_xattn_rms_scale, L0_xattn_q_w, L0_xattn_kv_w, L0_xattn_out_w, L0_ffn_in_proj_w, L0_ffn_in_proj_b, L0_ffn_out_w, L0_ffn_out_b, L0_ffn_gate_w, L0_ffn_gate_b, L0_ffn_w1, L0_ffn_b1, L0_ffn_w2, L0_ffn_b2, L0_ffn_ln1_g, L0_ffn_ln1_b, L0_ffn_ln2_g, L0_ffn_ln2_b):
    import jax
    import jax.numpy as jnp

    def _L0_xattn_ref(x, mem_seq, mem_mask, rms_scale, q_w, kv_w, out_w):
        import jax, jax.numpy as jnp
        import numpy as np
        NUM_HEADS, NUM_KV, HEAD_DIM, WIDTH = (4, 1, 32, 128)
        MASK_FILL = -2.3819763e+38

        def _apply_rope(x, positions, max_wavelength=10000.0):
            d = x.shape[-1]
            freq_exp = 2.0 / d * jnp.arange(d // 2, dtype=jnp.float32)
            timescale = max_wavelength ** freq_exp
            radians = positions[..., None].astype(jnp.float32) / timescale
            radians = radians[..., None, :]
            sin, cos = (jnp.sin(radians), jnp.cos(radians))
            x1, x2 = jnp.split(x, 2, axis=-1)
            out = jnp.concatenate([x1 * cos - x2 * sin, x2 * cos + x1 * sin], axis=-1)
            return out.astype(x.dtype)

        def _rmsnorm(x, scale):
            var = jnp.mean(jnp.square(x.astype(jnp.float32)), axis=-1, keepdims=True)
            normed = x * jax.lax.rsqrt(var + 1e-06)
            return (normed * (1 + scale)).astype(x.dtype)
        B, S, _ = mem_seq.shape
        T = x.shape[1]
        G = NUM_HEADS // NUM_KV
        xn = _rmsnorm(x, rms_scale)
        mn = _rmsnorm(mem_seq, rms_scale)
        q = jnp.einsum('BTD,NDH->BTNH', xn, q_w)
        kv = jnp.einsum('BSD,cKDH->cBSKH', mn, kv_w)
        k, v = (kv[0], kv[1])
        q_pos = jnp.broadcast_to(jnp.arange(S, T + S), (B, T))
        k_pos = jnp.broadcast_to(jnp.arange(S), (B, S))
        q = _apply_rope(q, q_pos) * HEAD_DIM ** (-0.5)
        k = _apply_rope(k, k_pos)
        q = q.reshape(B, T, NUM_KV, G, HEAD_DIM)
        logits = jnp.einsum('BTKGH,BSKH->BKGTS', q, k, preferred_element_type=jnp.float32)
        masked = jnp.where(mem_mask[:, None, None, None, :], logits, MASK_FILL)
        probs = jax.nn.softmax(masked, axis=-1).astype(x.dtype)
        enc = jnp.einsum('BKGTS,BSKH->BTKGH', probs, v).reshape(B, T, NUM_HEADS, HEAD_DIM)
        return jnp.einsum('BTNH,NHD->BTD', enc, out_w)

    def _L0_ffn_ref(src, in_proj_w, in_proj_b, out_w, out_b, gate_w, gate_b, w1, b1, w2, b2, ln1_g, ln1_b, ln2_g, ln2_b):
        import jax, jax.numpy as jnp
        import numpy as np
        S, B, D, H, E, K, F = (128, 4, 128, 16, 8, 2, 512)

        def _ln(x, g, b, eps=1e-05):
            mu = jnp.mean(x, axis=-1, keepdims=True)
            var = jnp.mean((x - mu) ** 2, axis=-1, keepdims=True)
            return (x - mu) * jax.lax.rsqrt(var + eps) * g + b
        s_len, bsz, d = src.shape
        dh = d // H
        qkv = src @ in_proj_w.T + in_proj_b
        q, k, v = jnp.split(qkv, 3, axis=-1)
        q = q.reshape(s_len, bsz, H, dh)
        k = k.reshape(s_len, bsz, H, dh)
        v = v.reshape(s_len, bsz, H, dh)
        scale = dh ** (-0.5)
        scores = jnp.einsum('sbhd,tbhd->bhst', q, k) * scale
        attn = jax.nn.softmax(scores, axis=-1)
        ctx = jnp.einsum('bhst,tbhd->sbhd', attn, v).reshape(s_len, bsz, d)
        attn_out = ctx @ out_w.T + out_b
        x = _ln(src + attn_out, ln1_g, ln1_b)
        tok = x.reshape(-1, d)
        n_tok = tok.shape[0]
        logits = tok @ gate_w.T + gate_b
        probs = jax.nn.softmax(logits, axis=-1)
        topv, topi = jax.lax.top_k(probs, K)
        topv = topv / jnp.sum(topv, axis=-1, keepdims=True)
        combine = jnp.zeros_like(probs).at[jnp.arange(n_tok)[:, None], topi].set(topv)
        moe_out = jnp.zeros_like(tok)
        for e in range(E):
            h = jax.nn.relu(tok @ w1[e].T + b1[e]) @ w2[e].T + b2[e]
            moe_out = moe_out + combine[:, e:e + 1] * h
        moe_out = moe_out.reshape(s_len, bsz, d)
        return _ln(x + moe_out, ln2_g, ln2_b)
    x = x + _L0_xattn_ref(_layernorm(x, axis=-1), ctx_1024, mask_BxS2_bk0, L0_xattn_rms_scale, L0_xattn_q_w, L0_xattn_kv_w, L0_xattn_out_w)
    x = x + _L0_ffn_ref(_layernorm(x, axis=-1), L0_ffn_in_proj_w, L0_ffn_in_proj_b, L0_ffn_out_w, L0_ffn_out_b, L0_ffn_gate_w, L0_ffn_gate_b, L0_ffn_w1, L0_ffn_b1, L0_ffn_w2, L0_ffn_b2, L0_ffn_ln1_g, L0_ffn_ln1_b, L0_ffn_ln2_g, L0_ffn_ln2_b)
    return x

_drawn_inputs = setup_inputs


def setup_inputs(seed=0):
    import zlib

    import numpy as np

    out = dict(_drawn_inputs(seed))
    spreads = {'L0_ffn_in_proj_b': (0.0, 0.617),
     'L0_ffn_out_b': (0.0, 0.269),
     'L0_ffn_gate_b': (0.0, 0.288),
     'L0_ffn_b1': (0.0, 0.8),
     'L0_ffn_b2': (0.0, 0.276),
     'L0_ffn_ln1_g': (1.0, 0.2),
     'L0_ffn_ln1_b': (0.0, 0.1),
     'L0_ffn_ln2_g': (1.0, 0.2),
     'L0_ffn_ln2_b': (0.0, 0.1)}
    factors = {'L0_xattn_rms_scale': 4.29,
     'L0_ffn_in_proj_w': 8.0,
     'L0_ffn_out_w': 4.713,
     'L0_ffn_w1': 2.806}
    for name, (base, spread) in spreads.items():
        noise = np.random.default_rng([zlib.crc32(name.encode()), seed]).standard_normal(out[name].shape)
        drawn = base * np.exp(spread * noise) if base else spread * noise
        out[name] = jnp.asarray(drawn.astype(out[name].dtype))
    for name, factor in factors.items():
        out[name] = (out[name] * factor).astype(out[name].dtype)
    return out
```

```python
from contextlib import ExitStack

import numpy as np

import concourse.bass as bass
from concourse import mybir

F32 = mybir.dt.float32
F32R = mybir.dt.float32r
BF16 = mybir.dt.bfloat16
U8 = mybir.dt.uint8
U32 = mybir.dt.uint32
ALU = mybir.AluOpType
ACT = mybir.ActivationFunctionType
AX_X = mybir.AxisListType.X

P = 128
D = 128
S = 32
T = 128
NH, HD = 4, 32
FH, FD = 16, 8
QUAD = 4
E, F, FC = 8, 512, 4
ROUTE = 17
GB = 4
NG = S // GB
CT = 16
NC = T // CT
TOK = 512
NQ = CT // 4
FILL = 2.3819763e38
EPS_LN, EPS_RMS = 1e-5, 1e-6
V_B1, V_B2, V_INB, V_G1, V_BE1, V_RMS, V_GATE, V_ROWS = 0, 32, 40, 43, 44, 45, 46, 54


def run_steps(eng, n, step):
    step(0, 0, True, False)
    with eng.Fori(0, (n - 2) // 2) as i:
        step(i * 2 + 1, 1, False, False)
        step(i * 2 + 2, 0, False, False)
    step(n - 1, (n - 1) % 2, False, True)


def build(nc, a, out):
    with ExitStack() as whole:
        def sb(name, shape, dt=F32, ctx=whole):
            return ctx.enter_context(nc.sbuf_tensor(name, shape, dt))

        def sem(name):
            return whole.enter_context(nc.semaphore(name))

        dram_res = nc.dram_tensor("residuals", [S, T, 2, D], F32, kind="Internal").ap()

        ident = sb("ident", [P, P])
        q_all = sb("q_all", [P, T, S])
        k_all = sb("k_all", [P, T, S])
        src_all = sb("src_all", [P, T, S])
        w1_hi = sb("w1_hi", [P, E * F], F32R)
        w1_lo = sb("w1_lo", [P, E * F], F32R)
        w2_t = sb("w2_t", [P, E * FC, D])
        proj_t = sb("proj_t", [P, 4, P])
        vec = sb("vec", [P, V_ROWS])
        q_bias = sb("q_bias", [P, 1])
        sel_bf = sb("sel_bf", [3 * E, E, P], BF16)
        ident_bf = sb("ident_bf", [P, P], BF16)
        held = sb("held", [P, 8])
        neg_half = sb("neg_half", [P, 8])
        psum = [whole.enter_context(nc.psum_tensor(f"bank{i}", [P, TOK], F32)) for i in range(4)]
        ps_s = whole.enter_context(nc.psum_tensor("bank_s", [P, 4, TOK], F32))

        block_a(nc, a, sem, psum, ps_s, locals())
        block_b(nc, a, out, sem, psum, ps_s, locals())


def block_a(nc, a, sem, psum, ps_s, m):
    sel_bf, ident_bf = m["sel_bf"], m["ident_bf"]
    held = m["held"]
    ident, q_all, k_all, src_all = m["ident"], m["q_all"], m["k_all"], m["src_all"]
    w1_hi, w1_lo, w2_t, proj_t, vec = m["w1_hi"], m["w1_lo"], m["w2_t"], m["proj_t"], m["vec"]
    q_bias, neg_half, dram_res = m["q_bias"], m["neg_half"], m["dram_res"]
    f0, f1, f2, r0 = psum
    with ExitStack() as ctx:
        def sb(name, shape, dt=F32):
            return ctx.enter_context(nc.sbuf_tensor(name, shape, dt))

        x_all = sb("x_all", [P, S, D])
        c_all = sb("c_all", [P, S, D])
        rope = sb("rope", [P, 4, T])
        vec_rows = sb("vec_rows", [V_ROWS, P])
        proj_rows = sb("proj_rows", [P, 4, P])
        wq_raw = sb("wq_raw", [P, NH, HD])
        kv_raw = sb("kv_raw", [P, 2, HD])
        wo_x = sb("wo_x", [P, D])
        rms1 = sb("rms1", [P, 1])
        wq = sb("wq", [P, NH, HD])
        wq_sw = sb("wq_sw", [P, NH, 2, HD // 2])
        wk = sb("wk", [P, NH, HD])
        wk_sw = sb("wk_sw", [P, NH, 2, HD // 2])
        wv = sb("wv", [P, HD])
        mask_u8 = sb("mask_u8", [P, S * T], U8)
        mask_g = sb("mask_g", [P, 2, TOK], BF16)
        ones_bf = sb("ones_bf", [P, P], BF16)
        stats = sb("stats", [P, 8, 6])
        mv = sb("mv", [P, 8, 2])
        msq = sb("msq", [P, 4])
        var_in = sb("var_in", [P, 8])
        rstd_in = sb("rstd_in", [P, 8])
        xn = sb("xn", [P, GB, D])
        mn = sb("mn", [P, GB, D])
        xn_t = sb("xn_t", [P, TOK])
        mn_t = sb("mn_t", [P, TOK])
        q_cos = sb("q_cos", [P, TOK])
        q_sin = sb("q_sin", [P, TOK])
        k_cos = sb("k_cos", [P, TOK])
        k_sin = sb("k_sin", [P, TOK])
        q_r = sb("q_r", [P, 2, GB, T])
        k_r = sb("k_r", [P, 2, GB, T])
        v_tok = sb("v_tok", [P, 2, GB, HD])
        neg_max = sb("neg_max", [P, NH, GB])
        row_sum = sb("row_sum", [P, NH, GB])
        row_rec = sb("row_rec", [P, NH, GB])
        probs = sb("probs", [P, NH, GB, T])
        probs_t = sb("probs_t", [P, NH, GB, T])
        enc_t = sb("enc_t", [P, TOK])
        x1 = sb("x1", [P, 2, GB, 2, D])
        sel_f = x1[0:3 * E, 1].rearrange("p b two d -> p (b two) d")
        stats1 = sb("stats1", [P, GB, 6])
        mv1 = sb("mv1", [P, GB, 2])
        var1 = sb("var1", [P, GB])
        rstd1 = sb("rstd1", [P, GB])
        src_t = sb("src_t", [P, TOK])

        ld_x = [sem(f"ld_x{i}") for i in range(2)]
        ld_w = [sem(f"ld_w{i}") for i in range(5)]
        vec_ps, vec_sb = sem("vec_ps"), sem("vec_sb")
        small_w = sem("small_w")
        small_a = sem("small_a")
        w_ps, w_hi_sb, w_lo_sb = sem("w_ps"), sem("w_hi_sb"), sem("w_lo_sb")
        in_stats, in_mv, in_var, in_rstd = sem("in_stats"), sem("in_mv"), sem("in_var"), sem("in_rstd")
        xn_sb, mn_sb = sem("xn_sb"), sem("mn_sb")
        xt_ps, mt_ps, xt_sb, mt_sb = sem("xt_ps"), sem("mt_ps"), sem("xt_sb"), sem("mt_sb")
        fq_ps, fqs_ps, fk_ps, fks_ps, fv_ps = (sem(n) for n in ("fq_ps", "fqs_ps", "fk_ps", "fks_ps", "fv_ps"))
        mask_rdy = sem("mask_rdy")
        rq, rk = sem("rq"), sem("rk")
        q_rdy, k_rdy, v_sb = sem("q_rdy"), sem("k_rdy"), sem("v_sb")
        sc_ps, max_sb, exp_sb, rec_sb, prob_sb = (sem(n) for n in ("sc_ps", "max_sb", "exp_sb", "rec_sb", "prob_sb"))
        pt_ps, pt_act, pt_dve = sem("pt_ps"), sem("pt_act"), sem("pt_dve")
        enc_ps, enc_sb, op_ps, x1_sb = sem("enc_ps"), sem("enc_sb"), sem("op_ps"), sem("x1_sb")
        st1, mv1_s, var1_s, rstd1_s, src_sb = (sem(n) for n in ("st1", "mv1_s", "var1_s", "rstd1_s", "src_sb"))
        stored = [sem(f"stored{i}") for i in range(2)]
        srct_ps, srct_sb, bq_ps, bq_sb, bk_ps, bk_sb = (
            sem(n) for n in ("srct_ps", "srct_sb", "bq_ps", "bq_sb", "bk_ps", "bk_sb"))

        w1_rows = q_all[:, :, :].rearrange("p a b -> p (a b)").rearrange("p (n d) -> p n d", d=D)
        w2_rows = k_all[:, :, :].rearrange("p a b -> p (a b)").rearrange("p (e f) -> p e f", e=E)
        res_g = dram_res.rearrange("(g b) t two d -> g t b two d", b=GB)
        x_g = a["x"].rearrange("(g b) t d -> g t b d", b=GB)
        c_g = a["ctx"].rearrange("(g b) t d -> g t b d", b=GB)

        def seqs(tile, g):
            return tile[:, bass.ts(g, GB), :]

        def ts_of(tile, g):
            return tile[:, :, bass.ts(g, GB)].rearrange("p t s -> p s t")

        block = ctx.enter_context(nc.Block())

        @block.sync
        def _(sp):
            sp.dma_start(ident[:, :], a["ident"]).then_inc(ld_w[0], 16)
            for row, n, src in ((V_B1, 32, a["b1"].rearrange("e (c f) -> (e c) f", c=FC)), (V_B2, E, a["b2"]),
                                (V_INB, 3, a["in_b"].rearrange("(c f) -> c f", c=3)),
                                (V_G1, 1, a["ln1_g"].rearrange("(a f) -> a f", a=1)),
                                (V_BE1, 1, a["ln1_b"].rearrange("(a f) -> a f", a=1)),
                                (V_RMS, 1, a["rms"].rearrange("(a f) -> a f", a=1)), (V_GATE, E, a["gate_w"])):
                sp.dma_start(vec_rows[row:row + n, :], src).then_inc(ld_w[0], 16)
            for g in range(NG):
                if g >= 2:
                    sp.wait_ge(ld_x[g % 2], g // 2 * 32)
                sp.dma_start(seqs(x_all, g), x_g[g]).then_inc(ld_x[g % 2], 16)
                sp.dma_start(seqs(c_all, g), c_g[g]).then_inc(ld_x[g % 2], 16)

            def step(g, p, first, last):
                sp.wait_ge(src_sb, g * GB + GB)
                sp.dma_start(res_g[g], x1[:, p]).then_inc(stored[p], 16)

            run_steps(sp, NG, step)
            for p in range(2):
                sp.wait_ge(stored[p], 16 * NG // 2)

        @block.scalar
        def _(act):
            act.dma_start(proj_rows[:, 0:3, :], a["in_w"].rearrange("(c j) d -> j c d", c=3)).then_inc(ld_w[1], 16)
            act.dma_start(proj_rows[:, 3, :], a["out_w"]).then_inc(ld_w[1], 16)
            act.dma_start(wq_raw[:, :, :], a["q_w"].rearrange("n d h -> d n h")).then_inc(ld_w[1], 16)
            act.dma_start(kv_raw[:, :, :], a["kv_w"].rearrange("c k d h -> d (c k) h")).then_inc(ld_w[1], 16)
            act.dma_start(wo_x[:, :], a["wo_x"].rearrange("n h d -> (n h) d")).then_inc(ld_w[1], 16)
            act.dma_start(rope[:, :, :], a["rope"].rearrange("n p t -> p n t")).then_inc(ld_w[2], 16)
            act.dma_start(sel_f[:, :, :], a["expert_sel"]).then_inc(ld_w[2], 16)
            act.dma_start(mask_u8[:, :], a["mask"].rearrange("s t -> (s t)").unsqueeze(0).to_broadcast([P, S * T])
                          ).then_inc(ld_w[2], 16)
            act.dma_start(w1_rows, a["w1"].rearrange("e (c f) d -> f (e c) d", c=FC)).then_inc(ld_w[3], 16)
            act.dma_start(w2_rows, a["w2"].rearrange("e d f -> d e f")).then_inc(ld_w[4], 16)
            act.wait_ge(vec_ps, 1)
            nc.scalar.activation(vec[:, :], r0[:, 0:V_ROWS], ACT.Copy).then_inc(vec_sb, 1)
            act.wait_ge(vec_ps, 2)
            nc.scalar.activation(proj_t[:, :, :], f0[:, :], ACT.Copy).then_inc(vec_sb, 1)
            banks = [f1, f2, ps_s[:, 0], ps_s[:, 1], ps_s[:, 2], ps_s[:, 3]]
            for n in range(16):
                act.wait_ge(w_ps, n + 1)
                dst = w1_hi[:, n * TOK:(n + 1) * TOK] if n < 8 else w2_t[:, (n - 8) * FC:(n - 7) * FC, :]
                nc.scalar.activation(dst, banks[n % 6][:, :], ACT.Copy).then_inc(w_hi_sb, 1)

            def norm_ctx(g):
                act.wait_ge(in_rstd, g + 1)
                if not isinstance(g, int) or g > 0:
                    act.wait_ge(mt_ps, g)
                for b in range(GB):
                    nc.scalar.activation(mn[:, b, :], c_all[:, g * GB + b, :], ACT.Copy,
                                         scale=rstd_in[:, GB + b:GB + b + 1]).then_inc(mn_sb, 1)

            def evac_front(g):
                act.wait_ge(xt_ps, g + 1)
                if not isinstance(g, int) or g > 0:
                    act.wait_ge(fqs_ps, g)
                nc.scalar.activation(xn_t[:, :], f0[:, :], ACT.Copy).then_inc(xt_sb, 1)
                act.wait_ge(mt_ps, g + 1)
                if not isinstance(g, int) or g > 0:
                    act.wait_ge(fv_ps, g)
                nc.scalar.activation(mn_t[:, :], f1[:, :], ACT.Copy).then_inc(mt_sb, 1)

            def evac_v(g, p):
                act.wait_ge(fv_ps, g + 1)
                if not isinstance(g, int) or g > 1:
                    act.wait_ge(enc_ps, g - 1)
                nc.scalar.activation(v_tok[:, p, :, :], f0[:, 0:GB * HD], ACT.Copy).then_inc(v_sb, 1)

            def evac_src(g):
                act.wait_ge(srct_ps, g + 1)
                nc.scalar.activation(src_t[:, :], r0[:, :], ACT.Copy).then_inc(srct_sb, 1)
                nc.scalar.activation(ts_of(src_all, g), r0[:, :].rearrange("p (s t) -> p s t", s=GB), ACT.Copy
                                     ).then_inc(srct_sb, 1)

            def evac_bq(g):
                act.wait_ge(bq_ps, g + 1)
                act.wait_ge(small_w, 7)
                nc.scalar.activation(ts_of(q_all, g), r0[:, :].rearrange("p (s t) -> p s t", s=GB), ACT.Identity,
                                     bias=q_bias[:, 0:1], scale=FD ** -0.5).then_inc(bq_sb, 1)

            norm_ctx(0)
            evac_front(0)
            evac_v(0, 0)

            def step(g, p, first, last):
                if not first:
                    evac_src(g - 1)
                if not last:
                    norm_ctx(g + 1)
                    evac_front(g + 1)
                if not first:
                    evac_bq(g - 1)
                for h in range(NH):
                    act.wait_ge(max_sb, g * NH + h + 1)
                    if not first:
                        act.wait_ge(pt_ps, g * NH - NH + h + 1)
                        act.wait_ge(rec_sb, g * NH - NH + h + 1)
                    for b in range(GB):
                        nc.scalar.activation(probs[:, h, b, :], ps_s[:, h, b * T:(b + 1) * T], ACT.Exp,
                                             bias=neg_max[:, h, b:b + 1], accum_out=row_sum[:, h, b:b + 1]
                                             ).then_inc(exp_sb, 1)
                if not last:
                    evac_v(g + 1, 1 - p)
                for h in range(2):
                    act.wait_ge(pt_ps, g * NH + h + 1)
                    if not first:
                        act.wait_ge(enc_ps, g)
                    nc.scalar.activation(probs_t[:, h, :, :], ps_s[:, h, :], ACT.Copy).then_inc(pt_act, 1)
                act.wait_ge(enc_ps, g + 1)
                if not first:
                    act.wait_ge(op_ps, g)
                nc.scalar.activation(enc_t[:, :], r0[:, :], ACT.Copy).then_inc(enc_sb, 1)

            run_steps(act, NG, step)
            evac_src(NG - 1)
            evac_bq(NG - 1)

        @block.vector
        def _(dve):
            nc.vector.memset(ones_bf[:, :], 1.0).then_inc(small_w, 1)
            nc.vector.memset(neg_half[:, :], -0.5).then_inc(small_w, 1)
            dve.wait_ge(vec_sb, 1)
            dve.wait_ge(ld_w[1], 80)
            dve.wait_ge(ld_w[2], 48)
            nc.vector.tensor_scalar(rms1[:, :], vec[:, V_RMS:V_RMS + 1], 1.0, None, ALU.add).then_inc(small_w, 1)
            dve.wait_ge(small_w, 3)
            nc.vector.tensor_scalar(wq[:, :, :], wq_raw[:, :, :], rms1[:, 0:1], HD ** -0.5, ALU.mult, ALU.mult
                                    ).then_inc(small_w, 1)
            nc.vector.tensor_scalar(wk[:, :, :], kv_raw[:, 0:1, :].to_broadcast([P, NH, HD]), rms1[:, 0:1], None,
                                    ALU.mult).then_inc(small_w, 1)
            nc.vector.tensor_scalar(wv[:, :], kv_raw[:, 1, :], rms1[:, 0:1], None, ALU.mult).then_inc(small_w, 1)
            nc.vector.tensor_scalar(q_bias[:, :], vec[:, V_INB:V_INB + 1], FD ** -0.5, None, ALU.mult
                                    ).then_inc(small_w, 1)
            dve.wait_ge(small_w, 5)
            for half in range(2):
                for dst, src in ((wq_sw, wq), (wk_sw, wk)):
                    o = (1 - half) * (HD // 2)
                    nc.vector.tensor_copy(dst[:, :, half, :], src[:, :, o:o + HD // 2]).then_inc(small_w, 1)
            banks = [f1, f2, ps_s[:, 0], ps_s[:, 1], ps_s[:, 2], ps_s[:, 3]]
            for n in range(8):
                dve.wait_ge(w_hi_sb, n + 1)
                cols = slice(n * TOK, (n + 1) * TOK)
                nc.vector.tensor_tensor(w1_lo[:, cols], banks[n % 6][:, :], w1_hi[:, cols].bitcast(F32), ALU.subtract
                                        ).then_inc(w_lo_sb, 1)

            def hold(cell):
                nc.vector.memset(held[:, cell:cell + 1], 0.0)

            def stats_in(g, p):
                dve.wait_ge(ld_x[p], g * 16 + (32 - 16 * p))
                if not isinstance(g, int) or g > 0:
                    dve.wait_ge(in_mv, g * 8)
                for b in range(GB):
                    nc.vector.bn_stats(stats[:, b, :], x_all[:, g * GB + b, :]).then_inc(in_stats, 1)
                    nc.vector.bn_stats(stats[:, GB + b, :], c_all[:, g * GB + b, :]).then_inc(in_stats, 1)
                if not isinstance(g, int) or g > 0:
                    dve.wait_ge(in_var, g * 3)
                    dve.wait_ge(xn_sb, g * GB)
                dve.wait_ge(in_stats, g * 8 + 8)
                hold(0)
                for b in range(2 * GB):
                    nc.vector.bn_aggr(mv[:, b, :], stats[:, b, :]).then_inc(in_mv, 1)
                dve.wait_ge(in_mv, g * 8 + 8)
                if not isinstance(g, int) or g > 0:
                    dve.wait_ge(in_rstd, g)
                nc.vector.tensor_scalar(var_in[:, 0:GB], mv[:, 0:GB, 1], 1.0 + EPS_RMS, EPS_RMS * EPS_LN,
                                        ALU.mult, ALU.add).then_inc(in_var, 1)
                nc.vector.tensor_tensor(msq[:, :], mv[:, GB:, 0], mv[:, GB:, 0], ALU.mult).then_inc(in_var, 1)
                dve.wait_ge(in_var, g * 3 + 2)
                nc.vector.scalar_tensor_tensor(var_in[:, GB:], msq[:, :], EPS_RMS, mv[:, GB:, 1], ALU.add, ALU.add
                                               ).then_inc(in_var, 1)

            def norm_x(g):
                dve.wait_ge(in_rstd, g + 1)
                if not isinstance(g, int) or g > 0:
                    dve.wait_ge(xt_ps, g)
                for b in range(GB):
                    nc.vector.tensor_scalar(xn[:, b, :], x_all[:, g * GB + b, :], mv[:, b, 0:1], rstd_in[:, b:b + 1],
                                            ALU.subtract, ALU.mult).then_inc(xn_sb, 1)

            def rotate(g):
                def table(n):
                    return rope[:, n:n + 1, :].to_broadcast([P, GB, T])

                def cols(t):
                    return t[:, :].rearrange("p (s t) -> p s t", s=GB)

                if not isinstance(g, int) or g > 0:
                    dve.wait_ge(q_rdy, g)
                    dve.wait_ge(k_rdy, g)
                dve.wait_ge(fq_ps, g + 1)
                nc.vector.tensor_tensor(cols(q_cos), cols(f2), table(0), ALU.mult).then_inc(rq, 1)
                dve.wait_ge(fqs_ps, g + 1)
                nc.vector.tensor_tensor(cols(q_sin), cols(f0), table(1), ALU.mult).then_inc(rq, 1)
                dve.wait_ge(fk_ps, g + 1)
                nc.vector.tensor_tensor(cols(k_cos), cols(f1), table(2), ALU.mult).then_inc(rk, 1)
                dve.wait_ge(fks_ps, g + 1)
                nc.vector.tensor_tensor(cols(k_sin), cols(f2), table(3), ALU.mult).then_inc(rk, 1)

            def evac_bk(g):
                dve.wait_ge(bk_ps, g + 1)
                nc.vector.tensor_scalar(ts_of(k_all, g), r0[:, :].rearrange("p (s t) -> p s t", s=GB),
                                        vec[:, V_INB + 1:V_INB + 2], None, ALU.add).then_inc(bk_sb, 1)

            def mask_of(g, p):
                nc.vector.tensor_scalar(mask_g[:, p, :], mask_u8[:, bass.ts(g, TOK)], FILL, -FILL, ALU.mult, ALU.add
                                        ).then_inc(mask_rdy, 1)

            mask_of(0, 0)
            stats_in(0, 0)
            norm_x(0)
            rotate(0)

            def step(g, p, first, last):
                if not last:
                    mask_of(g + 1, 1 - p)
                    stats_in(g + 1, 1 - p)
                for h in range(NH):
                    dve.wait_ge(sc_ps, g * NH + h + 1)
                    if not first:
                        dve.wait_ge(exp_sb, g * 16 - 16 + 4 * h + 4)
                    nc.vector.tensor_reduce(neg_max[:, h, :], ps_s[:, h, :].rearrange("p (s t) -> p s t", s=GB),
                                            AX_X, ALU.max, negate=True).then_inc(max_sb, 1)
                if not last:
                    norm_x(g + 1)
                    rotate(g + 1)
                if not first:
                    evac_bk(g - 1)
                for h in range(NH):
                    dve.wait_ge(exp_sb, g * 16 + 4 * h + 4)
                    if not first:
                        dve.wait_ge(prob_sb, g * NH - NH + h + 1)
                    nc.vector.reciprocal(row_rec[:, h, :], row_sum[:, h, :]).then_inc(rec_sb, 1)
                    dve.wait_ge(rec_sb, g * NH + h + 1)
                    nc.vector.tensor_tensor(probs[:, h, :, :], probs[:, h, :, :],
                                            row_rec[:, h, :].unsqueeze(2).to_broadcast([P, GB, T]), ALU.mult
                                            ).then_inc(prob_sb, 1)
                for h in range(2, NH):
                    dve.wait_ge(pt_ps, g * NH + h + 1)
                    if not first:
                        dve.wait_ge(enc_ps, g)
                    nc.vector.tensor_copy(probs_t[:, h, :, :], ps_s[:, h, :]).then_inc(pt_dve, 1)
                dve.wait_ge(op_ps, g + 1)
                if not first:
                    dve.wait_ge(stored[1 - p], g * 8 + 8 * p)
                nc.vector.tensor_tensor(x1[:, p, :, 0, :], r0[:, :].rearrange("p (s d) -> p s d", s=GB),
                                        seqs(x_all, g), ALU.add).then_inc(x1_sb, 1)
                dve.wait_ge(x1_sb, g + 1)
                if not first:
                    dve.wait_ge(mv1_s, g * GB)
                for b in range(GB):
                    nc.vector.bn_stats(stats1[:, b, :], x1[:, p, b, 0, :]).then_inc(st1, 1)
                if not first:
                    dve.wait_ge(src_sb, g * GB)
                dve.wait_ge(st1, g * GB + GB)
                hold(1)
                for b in range(GB):
                    nc.vector.bn_aggr(mv1[:, b, :], stats1[:, b, :]).then_inc(mv1_s, 1)
                dve.wait_ge(mv1_s, g * GB + GB)
                nc.vector.tensor_scalar(var1[:, :], mv1[:, :, 1], EPS_LN, None, ALU.add).then_inc(var1_s, 1)
                dve.wait_ge(rstd1_s, g + 1)
                if not first:
                    dve.wait_ge(srct_ps, g)
                for b in range(GB):
                    nc.vector.tensor_scalar(x1[:, p, b, 1, :], x1[:, p, b, 0, :], mv1[:, b, 0:1], rstd1[:, b:b + 1],
                                            ALU.subtract, ALU.mult).then_inc(src_sb, 1)

            run_steps(dve, NG, step)
            evac_bk(NG - 1)

        @block.gpsimd
        def _(pool):
            def rstd_of_inputs(g):
                pool.wait_ge(in_var, g * 3 + 3)
                if not isinstance(g, int) or g > 0:
                    pool.wait_ge(xn_sb, g * GB)
                    pool.wait_ge(mn_sb, g * GB)
                nc.gpsimd.tensor_tensor(rstd_in[:, :], var_in[:, :], neg_half[:, :], ALU.pow).then_inc(in_rstd, 1)

            def rotated(g, p):
                pool.wait_ge(rq, g * 2 + 2)
                if not isinstance(g, int) or g > 1:
                    pool.wait_ge(sc_ps, g * NH - NH)
                nc.gpsimd.tensor_tensor(q_r[:, p, :, :], q_cos[:, :].rearrange("p (s t) -> p s t", s=GB),
                                        q_sin[:, :].rearrange("p (s t) -> p s t", s=GB), ALU.add).then_inc(q_rdy, 1)
                pool.wait_ge(rk, g * 2 + 2)
                nc.gpsimd.tensor_tensor(k_r[:, p, :, :], k_cos[:, :].rearrange("p (s t) -> p s t", s=GB),
                                        k_sin[:, :].rearrange("p (s t) -> p s t", s=GB), ALU.add).then_inc(k_rdy, 1)

            pool.wait_ge(ld_w[0], 16 * 8)
            pool.wait_ge(ld_w[2], 48)
            nc.gpsimd.tensor_copy(ident_bf[:, :], ident[:, :])
            nc.gpsimd.tensor_copy(sel_bf[:, :, :], sel_f[:, :, :])
            pool.wait_ge(small_w, 2)
            rstd_of_inputs(0)
            rotated(0, 0)

            def step(g, p, first, last):
                if not last:
                    rstd_of_inputs(g + 1)
                    rotated(g + 1, 1 - p)
                pool.wait_ge(var1_s, g + 1)
                nc.gpsimd.tensor_tensor(rstd1[:, :], var1[:, :], neg_half[:, 0:GB], ALU.pow).then_inc(rstd1_s, 1)

            run_steps(pool, NG, step)

        @block.tensor
        def _(pe):
            pe.wait_ge(ld_w[0], 16 * 8)
            nc.tensor.transpose(r0[:, 0:V_ROWS], vec_rows[:, :], ident[0:V_ROWS, 0:V_ROWS]).then_inc(vec_ps, 1)
            pe.wait_ge(ld_w[1], 80)
            for n in range(4):
                mm = nc.tensor.transpose(f0[:, n * P:(n + 1) * P], proj_rows[:, n, :], ident[:, :])
            mm.then_inc(vec_ps, 1)
            banks = [f1, f2, ps_s[:, 0], ps_s[:, 1], ps_s[:, 2], ps_s[:, 3]]
            for n in range(16):
                if n == 0:
                    pe.wait_ge(ld_w[3], 16)
                if n == 8:
                    pe.wait_ge(ld_w[4], 16)
                if n >= 6:
                    pe.wait_ge(w_hi_sb, n - 5)
                    pe.wait_ge(w_lo_sb, min(n - 5, 8))
                for c in range(FC):
                    src = w1_rows[:, n * FC + c, :] if n < 8 else w2_rows[:, n - 8, c * P:(c + 1) * P]
                    mm = nc.tensor.transpose(banks[n % 6][:, c * P:(c + 1) * P], src, ident[:, :])
                mm.then_inc(w_ps, 1)

            def front_transposes(g):
                pe.wait_ge(xn_sb, g * GB + GB)
                if not isinstance(g, int) or g > 0:
                    pe.wait_ge(v_sb, g)
                else:
                    pe.wait_ge(vec_sb, 2)
                    pe.wait_ge(w_hi_sb, 16)
                    pe.wait_ge(w_lo_sb, 8)
                for b in range(GB):
                    mm = nc.tensor.transpose(f0[:, b * P:(b + 1) * P], xn[:, b, :], ident[:, :])
                mm.then_inc(xt_ps, 1)
                pe.wait_ge(mn_sb, g * GB + GB)
                if not isinstance(g, int) or g > 0:
                    pe.wait_ge(rk, g * 2)
                for b in range(GB):
                    mm = nc.tensor.transpose(f1[:, b * P:(b + 1) * P], mn[:, b, :], ident[:, :])
                mm.then_inc(mt_ps, 1)

            def front_q(g):
                if isinstance(g, int) and g == 0:
                    pe.wait_ge(small_w, 11)
                pe.wait_ge(xt_sb, g + 1)
                nc.tensor.matmul(f2[:, :], wq[:, :, :], xn_t[:, :], start=True, stop=True).then_inc(fq_ps, 1)
                nc.tensor.matmul(f0[:, :], wq_sw[:, :, :, :], xn_t[:, :], start=True, stop=True).then_inc(fqs_ps, 1)
                pe.wait_ge(mt_sb, g + 1)
                nc.tensor.matmul(f1[:, :], wk[:, :, :], mn_t[:, :], start=True, stop=True).then_inc(fk_ps, 1)

            def front_kv(g):
                pe.wait_ge(rq, g * 2 + 1)
                nc.tensor.matmul(f2[:, :], wk_sw[:, :, :, :], mn_t[:, :], start=True, stop=True).then_inc(fks_ps, 1)
                pe.wait_ge(rq, g * 2 + 2)
                for b in range(GB):
                    mm = nc.tensor.matmul(f0[:, b * HD:(b + 1) * HD], mn_t[:, b * T:(b + 1) * T], wv[:, :],
                                          start=True, stop=True)
                mm.then_inc(fv_ps, 1)

            def back_transposes(g, p):
                pe.wait_ge(src_sb, g * GB + GB)
                for b in range(GB):
                    mm = nc.tensor.transpose(r0[:, b * P:(b + 1) * P], x1[:, p, b, 1, :], ident[:, :])
                mm.then_inc(srct_ps, 1)

            def back_q(g):
                pe.wait_ge(srct_sb, g * 2 + 2)
                nc.tensor.matmul(r0[:, :], proj_t[:, 0, :], src_t[:, :], start=True, stop=True).then_inc(bq_ps, 1)

            def back_k(g):
                pe.wait_ge(bq_sb, g + 1)
                nc.tensor.matmul(r0[:, :], proj_t[:, 1, :], src_t[:, :], start=True, stop=True).then_inc(bk_ps, 1)

            front_transposes(0)
            front_q(0)
            front_kv(0)

            def step(g, p, first, last):
                pe.wait_ge(mask_rdy, g + 1)
                pe.wait_ge(q_rdy, g + 1)
                pe.wait_ge(k_rdy, g + 1)
                if not first:
                    pe.wait_ge(pt_act, g * 2)
                    pe.wait_ge(pt_dve, g * 2)
                for h in range(NH):
                    rows = slice(h * HD, (h + 1) * HD)
                    for b in range(GB):
                        cols = slice(b * T, (b + 1) * T)
                        nc.tensor.matmul(ps_s[:, h, cols], ones_bf[h * HD:h * HD + 1, :],
                                         mask_g[h * HD:h * HD + 1, p, cols], start=True, stop=False)
                        mm = nc.tensor.matmul(ps_s[:, h, cols], q_r[rows, p, b, :], k_r[rows, p, b, :],
                                              start=False, stop=True)
                    mm.then_inc(sc_ps, 1)
                if not first:
                    back_transposes(g - 1, 1 - p)
                if not last:
                    front_transposes(g + 1)
                if not first:
                    back_q(g - 1)
                if not last:
                    front_q(g + 1)
                if not first:
                    back_k(g - 1)
                if not last:
                    front_kv(g + 1)
                for h in range(NH):
                    pe.wait_ge(prob_sb, g * NH + h + 1)
                    for b in range(GB):
                        mm = nc.tensor.transpose(ps_s[:, h, b * T:(b + 1) * T], probs[:, h, b, :], ident[:, :])
                    mm.then_inc(pt_ps, 1)
                pe.wait_ge(pt_act, g * 2 + 2)
                pe.wait_ge(pt_dve, g * 2 + 2)
                pe.wait_ge(v_sb, g + 1)
                if not first:
                    pe.wait_ge(bk_sb, g)
                for b in range(GB):
                    for h in range(NH):
                        mm = nc.tensor.matmul(r0[h * HD:(h + 1) * HD, b * T:(b + 1) * T], v_tok[:, p, b, :],
                                              probs_t[:, h, b, :], start=True, stop=True)
                mm.then_inc(enc_ps, 1)
                pe.wait_ge(enc_sb, g + 1)
                for b in range(GB):
                    mm = nc.tensor.matmul(r0[:, b * D:(b + 1) * D], enc_t[:, b * T:(b + 1) * T], wo_x[:, :],
                                          start=True, stop=True)
                mm.then_inc(op_ps, 1)

            run_steps(pe, NG, step)
            back_transposes(NG - 1, (NG - 1) % 2)
            back_q(NG - 1)
            back_k(NG - 1)


def block_b(nc, a, out, sem, psum, ps_s, m):
    sel_bf, ident_bf = m["sel_bf"], m["ident_bf"]
    held = m["held"]
    ident, q_all, k_all, src_all = m["ident"], m["q_all"], m["k_all"], m["src_all"]
    w1_hi, w1_lo, w2_t, proj_t, vec = m["w1_hi"], m["w1_lo"], m["w2_t"], m["proj_t"], m["vec"]
    neg_half, dram_res = m["neg_half"], m["dram_res"]
    h_ps = psum[0:2]
    y_ps, a_ps = psum[2], psum[3]
    with ExitStack() as ctx:
        def sb(name, shape, dt=F32):
            return ctx.enter_context(nc.sbuf_tensor(name, shape, dt))

        quad_mask = sb("quad_mask", [P, QUAD])
        row_mask = sb("row_mask", [P, QUAD])
        iota8 = sb("iota8", [P, NQ, E])
        out_bias = sb("out_bias", [P, D])
        gate_bias = sb("gate_bias", [P, E])
        g2 = sb("g2", [P, D])
        be2 = sb("be2", [P, D])
        q_c = sb("q_c", [P, 2, CT, S])
        s_c = sb("s_c", [P, CT, 4, S])
        k_bd = sb("k_bd", [P, CT, QUAD, S])
        v_bd = sb("v_bd", [P, CT, FH // QUAD, QUAD, FD])
        res = sb("res", [P, 2, NQ, 2, D])
        neg_max = sb("neg_max2", [P, 4, 16])
        row_sum = sb("row_sum2", [P, 4, 16])
        row_rec = sb("row_rec2", [P, 4, 16])
        ex = sb("ex", [P, 4, TOK])
        ex_t = sb("ex_t", [P, 4, TOK])
        ctx_tok = sb("ctx_tok", [P, NQ, D])
        ctx_t = sb("ctx_t", [P, TOK])
        stats = sb("stats2", [P, NQ, 6])
        mv = sb("mv2", [P, NQ, 2])
        var = sb("var2", [P, NQ])
        rstd = sb("rstd2", [P, NQ])
        y_hat = sb("y_hat", [P, NQ, D])
        tok_t = sb("tok_t", [P, 2, TOK])
        tok_hi = sb("tok_hi", [P, 2, TOK], F32R)
        tok_lo = sb("tok_lo", [P, 2, TOK], F32R)
        logit = sb("logit", [P, NQ, E])
        top = sb("top", [P, NQ, 8])
        top_i = sb("top_i", [P, NQ, 8], U32)
        top_f = sb("top_f", [P, NQ, 2])
        gap = sb("gap", [P, NQ])
        gap_e = sb("gap_e", [P, NQ])
        wt_den = sb("wt_den", [P, NQ])
        wt = sb("wt", [P, NQ, 2])
        pick = sb("pick", [P, 2, NQ, E])
        comb = sb("comb", [P, NQ, E])
        part_bf = sb("part_bf", [P, NQ, 3, E], BF16)
        rest = sb("rest", [P, 2, NQ, E])
        comb_t = sb("comb_t", [3 * E, 2, TOK], BF16)
        comb_b = sb("comb_b", [P, 2, TOK])
        hid = sb("hid", [P, 2, FC, TOK])
        term = sb("term", [P, 2, TOK])
        acc = sb("acc", [P, 2, TOK])
        stats3 = sb("stats3", [P, NQ, 6])
        mv3 = sb("mv3", [P, NQ, 2])
        var3 = sb("var3", [P, NQ])
        rstd3 = sb("rstd3", [P, NQ])
        o_hat = sb("o_hat", [P, NQ, D])

        ld_c = sem("ld_c")
        ld_q = [sem(f"ld_q{i}") for i in range(2)]
        ld_r = [sem(f"ld_r{i}") for i in range(2)]
        s_rdy = sem("s_rdy")
        kbd_rdy, v_ps, v_rdy = sem("kbd_rdy"), sem("v_ps"), sem("v_rdy")
        sc_ps, mx_sb, sub_sb, ex_sb, sum_sb, rec_sb = (sem("b_" + n) for n in ("sc", "mx", "sub", "ex", "sum", "rec"))
        pt_ps, pt_act, pt_dve = sem("b_pt_ps"), sem("b_pt_act"), sem("b_pt_dve")
        av_ps, ctx_sb, ct_ps, ct_sb, o_ps = (sem("b_" + n) for n in ("av_ps", "ctx_sb", "ct_ps", "ct_sb", "o_ps"))
        bias_in, yin_sb = sem("bias_in"), sem("yin_sb")
        st2, mv2_s, var2_s, rstd2_s, yh_sb = (sem("b_" + n) for n in ("st2", "mv2", "var2", "rstd2", "yh"))
        tt_ps, tok_sb, thi_sb, tlo_sb = (sem("b_" + n) for n in ("tt_ps", "tok", "thi", "tlo"))
        gap_sb = sem("gap_sb")
        g_ps, route, route_e, route_p = sem("g_ps"), sem("route"), sem("route_e"), sem("route_p")
        cmb_ps, cmb_sb = sem("cmb_ps"), sem("cmb_sb")
        cb_ps, cb_sb = sem("cb_ps"), sem("cb_sb")
        h_rdy, h_sb, y_rdy, term_sb, acc_sb = (sem("b_" + n) for n in ("h_ps", "h_sb", "y_ps", "term", "acc"))
        z_sb, z_ps = sem("z_sb"), sem("z_ps")
        st3, mv3_s, var3_s, rstd3_s, oh_sb, om_sb, of_sb = (
            sem("b_" + n) for n in ("st3", "mv3", "var3", "rstd3", "oh", "om", "of"))
        x1b_sb = sem("x1b_sb")
        sent = sem("sent")

        res_c = dram_res.rearrange("s (c q j) two d -> c j s q (two d)", q=NQ, j=4)
        out_c = out.rearrange("s (c q j) d -> c j s q d", q=NQ, j=4)
        block = ctx.enter_context(nc.Block())

        def later(g, k):
            return not isinstance(g, int) or g >= k

        @block.sync
        def _(sp):
            consts = [(quad_mask[:, :], a["quad_mask"]), (row_mask[:, :], a["row_mask"]),
                      (iota8[:, :, :], a["iota8"]),
                      (out_bias[:, :], a["out_b"].unsqueeze(0).to_broadcast([P, D])),
                      (gate_bias[:, :], a["gate_b"].unsqueeze(0).to_broadcast([P, E])),
                      (g2[:, :], a["ln2_g"].unsqueeze(0).to_broadcast([P, D])),
                      (be2[:, :], a["ln2_b"].unsqueeze(0).to_broadcast([P, D]))]
            assert len(consts) == 7

            def load_q(c, p):
                if later(c, 2):
                    sp.wait_ge(sc_ps, c * 4 - 4)
                sp.dma_start(q_c[:, p], q_all[:, bass.ts(c, CT), :]).then_inc(ld_q[p], 16)

            def load_res(c, p):
                for j in range(4):
                    sp.dma_start(res[j * S:(j + 1) * S, p, :, :, :].rearrange("s q two d -> s q (two d)"),
                                 res_c[c, j]).then_inc(ld_r[p], 16)

            def store(c, p):
                sp.wait_ge(of_sb, c + 1)
                for j in range(4):
                    sp.dma_start(out_c[c, j], res[j * S:(j + 1) * S, p, :, 0, :]).then_inc(sent, 16)

            for dst, src in consts:
                sp.dma_start(dst, src).then_inc(ld_c, 16)
            for c in range(2):
                load_q(c, c)
                load_res(c, c)
            with sp.Fori(0, (NC - 2) // 2) as i:
                for p in range(2):
                    load_q(i * 2 + (p + 2), p)
                    store(i * 2 + p, p)
                    sp.wait_ge(sent, (i * 2 + (p + 1)) * 64)
                    load_res(i * 2 + (p + 2), p)
            store(NC - 2, 0)
            store(NC - 1, 1)
            sp.wait_ge(sent, 64 * NC)

        @block.scalar
        def _(act):

            def exps(c, groups=range(4)):
                for g in groups:
                    act.wait_ge(sub_sb, c * 4 + g + 1)
                    nc.scalar.activation(ex[:, g, :], ex[:, g, :], ACT.Exp).then_inc(ex_sb, 1)

            def probs(c):
                for g in range(2):
                    act.wait_ge(pt_ps, c * 4 + g + 1)
                    if later(c, 1):
                        act.wait_ge(av_ps, c)
                    nc.scalar.activation(ex_t[:, g, :], ps_s[:, g, :], ACT.Copy).then_inc(pt_act, 1)

            def context(c):
                act.wait_ge(ct_ps, c + 1)
                if later(c, 1):
                    act.wait_ge(o_ps, c)
                nc.scalar.activation(ctx_t[:, :], ps_s[:, 1, :], ACT.Identity, bias=vec[:, V_INB + 2:V_INB + 3]
                                     ).then_inc(ct_sb, 1)

            def tokens(c, p):
                act.wait_ge(tt_ps, c + 1)
                if later(c, 2):
                    act.wait_ge(h_rdy, c * 32 - 32)
                nc.scalar.activation(tok_hi[:, p, :], ps_s[:, 3, :], ACT.Identity, bias=vec[:, V_BE1:V_BE1 + 1],
                                     scale=vec[:, V_G1:V_G1 + 1]).then_inc(thi_sb, 1)

            def route_exp(c):
                act.wait_ge(gap_sb, c + 1)
                nc.scalar.activation(gap_e[:, :], gap[:, :], ACT.Exp).then_inc(route_e, 1)

            def combine(c, p):
                act.wait_ge(cmb_ps, c + 1)
                if later(c, 2):
                    act.wait_ge(cb_ps, c * 8 - 7)
                nc.scalar.activation(comb_t[:, p, :], a_ps[0:3 * E, :].bitcast(BF16)[:, 0:TOK], ACT.Copy
                                     ).then_inc(cmb_sb, 1)

            def weights(c, e):
                act.wait_ge(cb_ps, c * 8 + e + 1)
                if later(c, 1) or e >= 2:
                    act.wait_ge(term_sb, c * 8 + e - 1)
                nc.scalar.activation(comb_b[:, e % 2, :], a_ps[:, :], ACT.Copy).then_inc(cb_sb, 1)

            def relus(c, e, half):
                for f in (2 * half, 2 * half + 1):
                    act.wait_ge(h_rdy, c * 32 + e * 4 + f + 1)
                    if later(c, 1) or e >= 2:
                        act.wait_ge(y_rdy, c * 8 + e - 1)
                    nc.scalar.activation(hid[:, e % 2, f, :], h_ps[f % 2][:, :], ACT.Relu,
                                         bias=vec[:, V_B1 + e * FC + f:V_B1 + e * FC + f + 1]).then_inc(h_sb, 1)

            exps(0)
            probs(0)
            context(0)
            tokens(0, 0)
            route_exp(0)

            def step(c, p, first, last):
                for e in range(E):
                    relus(c, e, 0)
                    if e == 2 and not last:
                        exps(c + 1, (0, 1))
                    if e == 5 and not last:
                        context(c + 1)
                    relus(c, e, 1)
                    if e:
                        weights(c, e - 1)
                    elif not first:
                        weights(c - 1, E - 1)
                    if e == 0:
                        combine(c, p)
                    if last:
                        continue
                    if e == 2:
                        exps(c + 1, (2, 3))
                    if e == 3:
                        probs(c + 1)
                    if e == 6:
                        tokens(c + 1, 1 - p)
                    if e == 7:
                        route_exp(c + 1)

            run_steps(act, NC, step)
            weights(NC - 1, E - 1)

        @block.vector
        def _(dve):
            dve.wait_ge(ld_c, 112)

            def hold(cell):
                nc.vector.memset(held[:, cell:cell + 1], 0.0)

            def keys(c):
                if later(c, 1):
                    dve.wait_ge(sc_ps, c * 4)
                for h in range(QUAD):
                    nc.vector.tensor_scalar(k_bd[:, :, h, :], k_all[:, bass.ts(c, CT), :], quad_mask[:, h:h + 1], None,
                                            ALU.mult).then_inc(kbd_rdy, 1)

            def repeat_tokens(c):
                if later(c, 1):
                    dve.wait_ge(v_ps, c * 4)
                nc.vector.tensor_copy(s_c[:, :, :, :], src_all[:, bass.ts(c, CT), :].unsqueeze(2).to_broadcast(
                    [P, CT, 4, S])).then_inc(s_rdy, 1)

            def values(c):
                mask = row_mask[:, :].unsqueeze(1).unsqueeze(3).to_broadcast([P, 16, QUAD, FD])
                for q in range(NQ):
                    dve.wait_ge(v_ps, c * 4 + q + 1)
                    if later(c, 1):
                        dve.wait_ge(av_ps, c)
                    nc.vector.tensor_tensor(
                        v_bd[:, q * 4:q * 4 + 4, :, :, :].rearrange("p t g h d -> p (t g) h d"),
                        ps_s[:, q, :].rearrange("p (n h d) -> p n h d", h=QUAD, d=FD), mask, ALU.mult
                    ).then_inc(v_rdy, 1)

            def softmax_in(c, groups=range(4)):
                for g in groups:
                    dve.wait_ge(sc_ps, c * 4 + g + 1)
                    if later(c, 1):
                        dve.wait_ge(sub_sb, c * 4 - 4 + g + 1)
                        dve.wait_ge(pt_ps, c * 4 - 4 + g + 1)
                    v = ps_s[:, g, :].rearrange("p (r s) -> p r s", s=S)
                    nc.vector.tensor_reduce(neg_max[:, g, :], v, AX_X, ALU.max, negate=True).then_inc(mx_sb, 1)
                    dve.wait_ge(mx_sb, c * 4 + g + 1)
                    nc.vector.tensor_tensor(ex[:, g, :].rearrange("p (r s) -> p r s", s=S), v,
                                            neg_max[:, g, :].unsqueeze(2).to_broadcast([P, 16, S]), ALU.add
                                            ).then_inc(sub_sb, 1)

            def sums(c):
                if later(c, 1):
                    dve.wait_ge(rec_sb, c)
                for g in range(4):
                    dve.wait_ge(ex_sb, c * 4 + g + 1)
                    nc.vector.tensor_reduce(row_sum[:, g, :], ex[:, g, :].rearrange("p (r s) -> p r s", s=S),
                                            AX_X, ALU.add).then_inc(sum_sb, 1)
                dve.wait_ge(sum_sb, c * 4 + 4)
                if later(c, 1):
                    dve.wait_ge(ctx_sb, c * 4)
                nc.vector.reciprocal(row_rec[:, :, :], row_sum[:, :, :]).then_inc(rec_sb, 1)

            def probs(c):
                for g in range(2, 4):
                    dve.wait_ge(pt_ps, c * 4 + g + 1)
                    if later(c, 1):
                        dve.wait_ge(av_ps, c)
                    nc.vector.tensor_copy(ex_t[:, g, :], ps_s[:, g, :]).then_inc(pt_dve, 1)

            def context(c):
                dve.wait_ge(av_ps, c + 1)
                dve.wait_ge(rec_sb, c + 1)
                if later(c, 1):
                    dve.wait_ge(ct_ps, c)
                for g in range(4):
                    cols = slice(g * 32, g * 32 + 32)
                    nc.vector.tensor_tensor(
                        ctx_tok[:, :, cols].rearrange("p q (h d) -> p q h d", h=QUAD),
                        ps_s[:, 0, :].rearrange("p (q n) -> p q n", q=NQ)[:, :, cols].rearrange(
                            "p q (h d) -> p q h d", h=QUAD),
                        row_rec[:, g, :].rearrange("p (q h) -> p q h", q=NQ).unsqueeze(3).to_broadcast(
                            [P, NQ, QUAD, FD]), ALU.mult).then_inc(ctx_sb, 1)

            def norm1(c, p):
                dve.wait_ge(o_ps, c + 1)
                dve.wait_ge(bias_in, c + 1)
                y_in = res[:, p, :, 1, :]
                nc.vector.tensor_tensor(y_in, ps_s[:, 2, :].rearrange("p (q d) -> p q d", q=NQ),
                                        res[:, p, :, 1, :], ALU.add).then_inc(yin_sb, 1)
                dve.wait_ge(yin_sb, c + 1)
                if later(c, 1):
                    dve.wait_ge(mv2_s, c * 4)
                    dve.wait_ge(yh_sb, c * 4)
                for q in range(NQ):
                    nc.vector.bn_stats(stats[:, q, :], y_in[:, q, :]).then_inc(st2, 1)
                dve.wait_ge(st2, c * 4 + 4)
                hold(2)
                for q in range(NQ):
                    nc.vector.bn_aggr(mv[:, q, :], stats[:, q, :]).then_inc(mv2_s, 1)
                dve.wait_ge(mv2_s, c * 4 + 4)
                nc.vector.tensor_scalar(var[:, :], mv[:, :, 1], EPS_LN, None, ALU.add).then_inc(var2_s, 1)

            def normed1(c, p):
                y_in = res[:, p, :, 1, :]
                dve.wait_ge(rstd2_s, c + 1)
                if later(c, 1):
                    dve.wait_ge(tt_ps, c)
                for q in range(NQ):
                    nc.vector.tensor_scalar(y_hat[:, q, :], y_in[:, q, :], mv[:, q, 0:1], rstd[:, q:q + 1],
                                            ALU.subtract, ALU.mult).then_inc(yh_sb, 1)

            def tokens(c, p):
                dve.wait_ge(tt_ps, c + 1)
                if later(c, 2):
                    dve.wait_ge(z_sb, c - 1)
                dve.wait_ge(thi_sb, c + 1)
                nc.vector.tensor_scalar(tok_t[:, p, :], ps_s[:, 3, :], vec[:, V_G1:V_G1 + 1], vec[:, V_BE1:V_BE1 + 1],
                                        ALU.mult, ALU.add).then_inc(tok_sb, 1)
                dve.wait_ge(tok_sb, c + 1)
                if later(c, 2):
                    dve.wait_ge(h_rdy, c * 32 - 32)
                nc.vector.tensor_tensor(tok_lo[:, p, :], tok_t[:, p, :], tok_hi[:, p, :].bitcast(F32), ALU.subtract
                                        ).then_inc(tlo_sb, 1)

            def routing(c):
                n = [0]

                def link(ins):
                    n[0] += 1
                    ins.then_inc(route, 1)
                    dve.wait_ge(route, c * ROUTE + n[0])

                dve.wait_ge(g_ps, c + 1)
                link(nc.vector.tensor_tensor(logit[:, :, :], ps_s[:, 0, 0:NQ * E].rearrange("p (q e) -> p q e", q=NQ),
                                             gate_bias[:, :].unsqueeze(1).to_broadcast([P, NQ, E]), ALU.add))
                hold(4)
                for q in range(NQ):
                    ins = nc.vector.max(top[:, q, :], logit[:, q, :])
                link(ins)
                nc.vector.tensor_tensor(gap[:, :], top[:, :, 1], top[:, :, 0], ALU.subtract).then_inc(gap_sb, 1)
                for q in range(NQ):
                    ins = nc.vector.max_index(top_i[:, q, :], top[:, q, :], logit[:, q, :])
                link(ins)
                link(nc.vector.tensor_copy(top_f[:, :, :], top_i[:, :, 0:2]))
                dve.wait_ge(route_e, c + 1)
                link(nc.vector.tensor_scalar(wt_den[:, :], gap_e[:, :], 1.0, None, ALU.add))
                link(nc.vector.reciprocal(wt[:, :, 0], wt_den[:, :]))
                link(nc.vector.tensor_tensor(wt[:, :, 1], wt[:, :, 0], gap_e[:, :], ALU.mult))
                for k in range(2):
                    link(nc.vector.tensor_tensor(pick[:, k, :, :], iota8[:, :, :],
                                                 top_f[:, :, k:k + 1].to_broadcast([P, NQ, E]), ALU.is_equal))
                for k in range(2):
                    link(nc.vector.tensor_tensor(pick[:, k, :, :], pick[:, k, :, :],
                                                 wt[:, :, k:k + 1].to_broadcast([P, NQ, E]), ALU.mult))
                link(nc.vector.tensor_tensor(comb[:, :, :], pick[:, 0, :, :], pick[:, 1, :, :], ALU.add))
                if later(c, 1):
                    dve.wait_ge(cmb_ps, c)
                link(nc.vector.tensor_copy(part_bf[:, :, 0, :], comb[:, :, :]))
                link(nc.vector.tensor_tensor(rest[:, 0, :, :], comb[:, :, :], part_bf[:, :, 0, :], ALU.subtract))
                link(nc.vector.tensor_copy(part_bf[:, :, 1, :], rest[:, 0, :, :]))
                link(nc.vector.tensor_tensor(rest[:, 1, :, :], rest[:, 0, :, :], part_bf[:, :, 1, :], ALU.subtract))
                link(nc.vector.tensor_copy(part_bf[:, :, 2, :], rest[:, 1, :, :]))
                assert n[0] == ROUTE

            def weigh(c, e, p):
                dve.wait_ge(y_rdy, c * E + e + 1)
                dve.wait_ge(cb_sb, c * E + e + 1)
                if e == 0:
                    pass
                elif e >= 3:
                    dve.wait_ge(acc_sb, c * (E - 1) + e - 2)
                elif later(c, 1):
                    dve.wait_ge(acc_sb, c * (E - 1))
                dst = acc[:, p, :] if e == 0 else term[:, e % 2, :]
                nc.vector.scalar_tensor_tensor(dst, y_ps[:, :], vec[:, V_B2 + e:V_B2 + e + 1], comb_b[:, e % 2, :],
                                               ALU.add, ALU.mult).then_inc(term_sb, 1)

            def finish(c, p):
                dve.wait_ge(z_ps, c + 1)
                z = a_ps[:, :].rearrange("p (q d) -> p q d", q=NQ)
                for q in range(NQ):
                    nc.vector.bn_stats(stats3[:, q, :], z[:, q, :]).then_inc(st3, 1)
                dve.wait_ge(st3, c * NQ + NQ)
                hold(3)
                for q in range(NQ):
                    nc.vector.bn_aggr(mv3[:, q, :], stats3[:, q, :]).then_inc(mv3_s, 1)
                dve.wait_ge(mv3_s, c * NQ + NQ)
                nc.vector.tensor_scalar(var3[:, :], mv3[:, :, 1], EPS_LN, None, ALU.add).then_inc(var3_s, 1)
                dve.wait_ge(rstd3_s, c + 1)
                for q in range(NQ):
                    nc.vector.tensor_scalar(o_hat[:, q, :], z[:, q, :], mv3[:, q, 0:1], rstd3[:, q:q + 1],
                                            ALU.subtract, ALU.mult).then_inc(oh_sb, 1)
                dve.wait_ge(oh_sb, c * NQ + NQ)
                nc.vector.tensor_tensor(o_hat[:, :, :], o_hat[:, :, :], g2[:, :].unsqueeze(1).to_broadcast([P, NQ, D]),
                                        ALU.mult).then_inc(om_sb, 1)
                dve.wait_ge(om_sb, c + 1)
                dve.wait_ge(x1b_sb, c + 1)
                nc.vector.tensor_tensor(res[:, p, :, 0, :], o_hat[:, :, :], res[:, p, :, 0, :], ALU.add
                                        ).then_inc(of_sb, 1)

            repeat_tokens(0)
            keys(0)
            values(0)
            softmax_in(0)
            sums(0)
            probs(0)
            context(0)
            norm1(0, 0)
            normed1(0, 0)
            tokens(0, 0)
            routing(0)

            def step(c, p, first, last):
                if not last:
                    repeat_tokens(c + 1)
                    keys(c + 1)
                if not first:
                    weigh(c - 1, 7, 1 - p)
                if not last:
                    values(c + 1)
                weigh(c, 0, p)
                if not last:
                    softmax_in(c + 1)
                weigh(c, 1, p)
                if not first:
                    finish(c - 1, 1 - p)
                if not last:
                    sums(c + 1)
                weigh(c, 2, p)
                if not last:
                    probs(c + 1)
                    context(c + 1)
                weigh(c, 3, p)
                if not last:
                    norm1(c + 1, 1 - p)
                weigh(c, 4, p)
                if not last:
                    normed1(c + 1, 1 - p)
                    tokens(c + 1, 1 - p)
                weigh(c, 5, p)
                weigh(c, 6, p)
                if not last:
                    routing(c + 1)

            run_steps(dve, NC, step)
            weigh(NC - 1, E - 1, 1)
            finish(NC - 1, 1)

        @block.gpsimd
        def _(pool):
            pool.wait_ge(ld_c, 112)

            def biases(c, p):
                pool.wait_ge(ld_r[p], c * 32 + (64 - 32 * p))
                nc.gpsimd.tensor_tensor(res[:, p, :, 1, :], res[:, p, :, 1, :],
                                        out_bias[:, :].unsqueeze(1).to_broadcast([P, NQ, D]), ALU.add
                                        ).then_inc(bias_in, 1)
                nc.gpsimd.tensor_tensor(res[:, p, :, 0, :], res[:, p, :, 0, :],
                                        be2[:, :].unsqueeze(1).to_broadcast([P, NQ, D]), ALU.add).then_inc(x1b_sb, 1)

            def rstd_1(c):
                pool.wait_ge(var2_s, c + 1)
                if later(c, 1):
                    pool.wait_ge(yh_sb, c * NQ)
                nc.gpsimd.tensor_tensor(rstd[:, :], var[:, :], neg_half[:, 0:NQ], ALU.pow).then_inc(rstd2_s, 1)

            def rstd_2(c):
                pool.wait_ge(var3_s, c + 1)
                nc.gpsimd.tensor_tensor(rstd3[:, :], var3[:, :], neg_half[:, 0:NQ], ALU.pow).then_inc(rstd3_s, 1)

            def add(c, e, p):
                pool.wait_ge(term_sb, c * E + e + 1)
                if later(c, 1) or e > 1:
                    pool.wait_ge(acc_sb, c * (E - 1) + e - 1)
                nc.gpsimd.tensor_tensor(acc[:, p, :], acc[:, p, :], term[:, e % 2, :], ALU.add).then_inc(acc_sb, 1)

            def residual(c, p):
                pool.wait_ge(acc_sb, (c + 1) * (E - 1))
                nc.gpsimd.tensor_tensor(acc[:, p, :], acc[:, p, :], tok_t[:, p, :], ALU.add).then_inc(z_sb, 1)

            biases(0, 0)
            rstd_1(0)

            def step(c, p, first, last):
                if not first:
                    add(c - 1, E - 1, 1 - p)
                    residual(c - 1, 1 - p)
                add(c, 1, p)
                if not first:
                    rstd_2(c - 1)
                add(c, 2, p)
                if not last:
                    biases(c + 1, 1 - p)
                add(c, 3, p)
                if not last:
                    rstd_1(c + 1)
                for e in range(4, E - 1):
                    add(c, e, p)

            run_steps(pool, NC, step)
            add(NC - 1, E - 1, 1)
            residual(NC - 1, 1)
            rstd_2(NC - 1)

        @block.tensor
        def _(pe):
            pe.wait_ge(ld_c, 112)

            def values(c):
                pe.wait_ge(s_rdy, c + 1)
                if later(c, 1):
                    pe.wait_ge(route, c * ROUTE - ROUTE + 1)
                for q in range(NQ):
                    for j in range(4):
                        mm = nc.tensor.matmul(ps_s[:, q, j * P:(j + 1) * P], s_c[:, q * 4 + j, :, :], proj_t[:, 2, :],
                                              start=True, stop=True)
                    mm.then_inc(v_ps, 1)

            def scores_wait(c, p):
                pe.wait_ge(ld_q[p], c * 8 + (16 - 8 * p))
                pe.wait_ge(kbd_rdy, c * QUAD + QUAD)
                pe.wait_ge(v_rdy, c * 4 + 4)

            def scores(c, p, q):
                for g in range(4):
                    rows = slice(g * 32, g * 32 + 32)
                    for j in range(4):
                        t = q * 4 + j
                        mm = nc.tensor.matmul(ps_s[j * S:(j + 1) * S, g, q * P:(q + 1) * P], q_c[rows, p, t, :],
                                              k_bd[rows, t, :, :], start=True, stop=True)
                    if q == NQ - 1:
                        mm.then_inc(sc_ps, 1)

            def probs(c, groups=range(4)):
                for g in groups:
                    pe.wait_ge(ex_sb, c * 4 + g + 1)
                    for q in range(NQ):
                        mm = nc.tensor.transpose(ps_s[:, g, q * P:(q + 1) * P], ex[:, g, q * P:(q + 1) * P], ident[:, :])
                    mm.then_inc(pt_ps, 1)

            def attend(c):
                pe.wait_ge(pt_act, c * 2 + 2)
                pe.wait_ge(pt_dve, c * 2 + 2)
                for q in range(NQ):
                    for g in range(4):
                        for j in range(4):
                            o = q * P + g * 32
                            mm = nc.tensor.matmul(ps_s[j * S:(j + 1) * S, 0, o:o + 32],
                                                  ex_t[:, g, q * P + j * S:q * P + (j + 1) * S],
                                                  v_bd[:, q * 4 + j, g, :, :], start=True, stop=True)
                mm.then_inc(av_ps, 1)

            def turn(bank, tile, done):
                for q in range(NQ):
                    mm = nc.tensor.transpose(bank[:, q * P:(q + 1) * P], tile[:, q, :], ident[:, :])
                mm.then_inc(done, 1)

            def context(c):
                pe.wait_ge(ctx_sb, c * 4 + 4)
                turn(ps_s[:, 1, :], ctx_tok, ct_ps)

            def out_proj(c):
                pe.wait_ge(ct_sb, c + 1)
                for q in range(NQ):
                    mm = nc.tensor.matmul(ps_s[:, 2, q * D:(q + 1) * D], ctx_t[:, q * P:(q + 1) * P], proj_t[:, 3, :],
                                          start=True, stop=True)
                mm.then_inc(o_ps, 1)

            def tokens(c):
                pe.wait_ge(yh_sb, c * NQ + NQ)
                turn(ps_s[:, 3, :], y_hat, tt_ps)

            def gate(c, p):
                pe.wait_ge(tok_sb, c + 1)
                for q in range(NQ):
                    mm = nc.tensor.matmul(ps_s[:, 0, q * E:(q + 1) * E], tok_t[:, p, q * P:(q + 1) * P],
                                          vec[:, V_GATE:V_GATE + E], start=True, stop=True)
                mm.then_inc(g_ps, 1)

            def combine(c):
                pe.wait_ge(route, c * ROUTE + ROUTE)
                if later(c, 1):
                    pe.wait_ge(cb_sb, c * E)
                dst = a_ps[0:3 * E, :].bitcast(BF16)
                for q in range(NQ):
                    mm = nc.tensor.transpose(dst[:, q * P:(q + 1) * P],
                                             part_bf[:, q, :, :].rearrange("p k e -> p (k e)"), ident_bf[:, :])
                mm.then_inc(cmb_ps, 1)

            def weights(c, e, p):
                if e == 0:
                    pe.wait_ge(cmb_sb, c + 1)
                else:
                    pe.wait_ge(cb_sb, c * E + e)
                if e == 2 and later(c, 1):
                    pe.wait_ge(oh_sb, c * NQ)
                nc.tensor.matmul(a_ps[:, :], sel_bf[:, e, :], comb_t[:, p, :], start=True, stop=True).then_inc(cb_ps, 1)

            def hidden(c, e, p, half, before_last=None):
                if e == 0 and half == 0:
                    pe.wait_ge(thi_sb, c + 1)
                    pe.wait_ge(tlo_sb, c + 1)
                for f in (2 * half, 2 * half + 1):
                    n = e * FC + f
                    if later(c, 1) or n >= 2:
                        pe.wait_ge(h_sb, c * E * FC + n - 1)
                    cols = slice(n * P, (n + 1) * P)
                    dst = h_ps[f % 2][:, :]
                    nc.tensor.matmul(dst, w1_hi[:, cols], tok_hi[:, p, :], start=True, stop=False)
                    nc.tensor.matmul(dst, w1_hi[:, cols], tok_lo[:, p, :], start=False, stop=False)
                    if f % 2 and before_last:
                        before_last()
                    nc.tensor.matmul(dst, w1_lo[:, cols], tok_hi[:, p, :], start=False, stop=True).then_inc(h_rdy, 1)

            def expert_out(c, e, half):
                if half == 0 and (later(c, 1) or e):
                    pe.wait_ge(term_sb, c * E + e)
                for f in (2 * half, 2 * half + 1):
                    n = e * FC + f
                    pe.wait_ge(h_sb, c * E * FC + n + 1)
                    mm = nc.tensor.matmul(y_ps[:, :], w2_t[:, n, :], hid[:, e % 2, f, :],
                                          start=(f == 0), stop=(f == FC - 1))
                if half:
                    mm.then_inc(y_rdy, 1)

            def sums(c, p):
                pe.wait_ge(z_sb, c + 1)
                pe.wait_ge(cb_sb, c * E + E + 2)
                for q in range(NQ):
                    mm = nc.tensor.transpose(a_ps[:, q * P:(q + 1) * P], acc[:, p, q * P:(q + 1) * P], ident[:, :])
                mm.then_inc(z_ps, 1)

            values(0)
            scores_wait(0, 0)
            for q in range(NQ):
                scores(0, 0, q)
            probs(0)
            attend(0)
            context(0)
            out_proj(0)
            tokens(0)
            gate(0, 0)

            def step(c, p, first, last):
                ahead = {
                    (0, 3): lambda: values(c + 1),
                    (1, 0): lambda: scores(c + 1, 1 - p, 0), (1, 1): lambda: scores(c + 1, 1 - p, 1),
                    (1, 2): lambda: scores(c + 1, 1 - p, 2), (1, 3): lambda: scores(c + 1, 1 - p, 3),
                    (3, 0): lambda: probs(c + 1, (0, 1)), (3, 2): lambda: probs(c + 1, (2, 3)),
                    (4, 1): lambda: attend(c + 1), (5, 0): lambda: context(c + 1), (5, 2): lambda: out_proj(c + 1),
                    (6, 2): lambda: tokens(c + 1), (7, 0): lambda: gate(c + 1, 1 - p)}

                def next_chunk(e, place):
                    if (e, place) in ahead and not last:
                        ahead[e, place]()

                for e in range(E):
                    before = (c, e - 1, p) if e else (c - 1, E - 1, 1 - p)
                    hidden(c, e, p, 0, (lambda: scores_wait(c + 1, 1 - p)) if e == 1 and not last else None)
                    next_chunk(e, 0)
                    if e or not first:
                        expert_out(before[0], before[1], 0)
                    next_chunk(e, 1)
                    hidden(c, e, p, 1)
                    next_chunk(e, 2)
                    if e or not first:
                        weights(*before)
                        expert_out(before[0], before[1], 1)
                    if e == 0:
                        combine(c)
                    if e == 2 and not first:
                        sums(c - 1, 1 - p)
                    next_chunk(e, 3)

            run_steps(pe, NC, step)
            expert_out(NC - 1, E - 1, 0)
            weights(NC - 1, E - 1, (NC - 1) % 2)
            expert_out(NC - 1, E - 1, 1)
            pe.wait_ge(z_sb, NC)
            pe.wait_ge(cb_sb, NC * E)
            for q in range(NQ):
                mm = nc.tensor.transpose(a_ps[:, q * P:(q + 1) * P], acc[:, 1, q * P:(q + 1) * P], ident[:, :])
            mm.then_inc(z_ps, 1)


_NAMES = {
    "x": "x", "ctx": "ctx_1024", "mask": "mask_BxS2_bk0", "rms": "L0_xattn_rms_scale", "q_w": "L0_xattn_q_w",
    "kv_w": "L0_xattn_kv_w", "wo_x": "L0_xattn_out_w", "in_w": "L0_ffn_in_proj_w", "in_b": "L0_ffn_in_proj_b",
    "out_w": "L0_ffn_out_w", "out_b": "L0_ffn_out_b", "gate_w": "L0_ffn_gate_w", "gate_b": "L0_ffn_gate_b",
    "w1": "L0_ffn_w1", "b1": "L0_ffn_b1", "w2": "L0_ffn_w2", "b2": "L0_ffn_b2", "ln1_g": "L0_ffn_ln1_g",
    "ln1_b": "L0_ffn_ln1_b", "ln2_g": "L0_ffn_ln2_g", "ln2_b": "L0_ffn_ln2_b",
}


def constants():
    half = HD // 2
    scale = np.float32(10000.0) ** (np.float32(2.0 / HD) * np.arange(half, dtype=np.float32))
    rope = np.zeros((4, P, T), np.float32)
    for n, first in ((0, T), (2, 0)):
        angle = (np.arange(first, first + T, dtype=np.float32)[:, None] / scale).T
        cos, sin = np.cos(angle), np.sin(angle)
        rope[n] = np.tile(np.concatenate([cos, cos]), (NH, 1))
        rope[n + 1] = np.tile(np.concatenate([-sin, sin]), (NH, 1))
    p = np.arange(P)
    sel = np.zeros((3 * E, E, P), np.float32)
    for r in range(3 * E):
        sel[r, r % E] = 1.0
    return {
        "ident": np.eye(P, dtype=np.float32), "rope": rope,
        "quad_mask": ((p % 32)[:, None] // FD == np.arange(QUAD)).astype(np.float32),
        "row_mask": (p[:, None] // 32 == np.arange(QUAD)).astype(np.float32),
        "expert_sel": sel,
        "iota8": np.broadcast_to(np.arange(E, dtype=np.float32), (P, NQ, E)).copy(),
    }


def kernel(**inputs):
    import concourse.bacc as bacc
    from concourse.bass_utils import run_bass_kernel_spmd

    nc = bacc.Bacc("TRN2", target_bir_lowering=False, num_devices=1)
    arrays, args = {}, {}
    given = {short: np.ascontiguousarray(inputs[name]) for short, name in _NAMES.items()}
    for name, array in {**given, **constants()}.items():
        arrays[f"in_{name}"] = array
        args[name] = nc.dram_tensor(f"in_{name}", array.shape, mybir.dt.from_np(array.dtype), kind="ExternalInput").ap()
    out = nc.dram_tensor("out_x", [S, T, D], F32, kind="ExternalOutput").ap()
    build(nc, args, out)
    r = run_bass_kernel_spmd(nc, [arrays], core_ids=[0])
    return r.results[0]["out_x"]
```

```python
from contextlib import ExitStack

import numpy as np

import concourse.bass as bass
from concourse import mybir

F32 = mybir.dt.float32
F32R = mybir.dt.float32r
BF16 = mybir.dt.bfloat16
U8 = mybir.dt.uint8
U32 = mybir.dt.uint32
ALU = mybir.AluOpType
ACT = mybir.ActivationFunctionType
AX_X = mybir.AxisListType.X

P = 128
D = 128
S = 32
T = 128
NH, HD = 4, 32
FH, FD = 16, 8
QUAD = 4
E, F, FC = 8, 512, 4
ROUTE = 17
GB = 4
NG = S // GB
CT = 16
NC = T // CT
TOK = 512
NQ = CT // 4
FILL = 2.3819763e38
EPS_LN, EPS_RMS = 1e-5, 1e-6
V_B1, V_B2, V_INB, V_G1, V_BE1, V_RMS, V_GATE, V_ROWS = 0, 32, 40, 43, 44, 45, 46, 54


def run_steps(eng, n, step):
    step(0, 0, True, False)
    with eng.Fori(0, (n - 2) // 2) as i:
        step(i * 2 + 1, 1, False, False)
        step(i * 2 + 2, 0, False, False)
    step(n - 1, (n - 1) % 2, False, True)


def build(nc, a, out):
    with ExitStack() as whole:
        def sb(name, shape, dt=F32, ctx=whole):
            return ctx.enter_context(nc.sbuf_tensor(name, shape, dt))

        def sem(name):
            return whole.enter_context(nc.semaphore(name))

        dram_q = nc.dram_tensor("queries", [S, P, T], F32, kind="Internal").ap()
        dram_res = nc.dram_tensor("residuals", [S, T, 2, D], F32, kind="Internal").ap()

        ident = sb("ident", [P, P])
        k_all = sb("k_all", [P, T, S])
        src_all = sb("src_all", [P, T, S])
        w1_hi = sb("w1_hi", [P, E * F], F32R)
        w1_lo = sb("w1_lo", [P, E * F], F32R)
        w2_hi = sb("w2_hi", [P, E, FC, D], F32R)
        w2_lo = sb("w2_lo", [P, E, FC, D], F32R)
        proj_t = sb("proj_t", [P, 4, P])
        vec = sb("vec", [P, V_ROWS])
        q_bias = sb("q_bias", [P, 1])
        quad_mask = sb("quad_mask", [P, QUAD])
        row_mask = sb("row_mask", [P, QUAD])
        iota8 = sb("iota8", [P, NQ, E])
        out_bias = sb("out_bias", [P, D])
        gate_bias = sb("gate_bias", [P, E])
        g2 = sb("g2", [P, D])
        be2 = sb("be2", [P, D])
        sel_bf = sb("sel_bf", [3 * E, E, P], BF16)
        ident_bf = sb("ident_bf", [P, P], BF16)
        held = sb("held", [P, 10])
        neg_half = sb("neg_half", [P, 8])
        psum = [whole.enter_context(nc.psum_tensor(f"bank{i}", [P, TOK], F32)) for i in range(4)]
        ps_s = whole.enter_context(nc.psum_tensor("bank_s", [P, 4, TOK], F32))

        block_a(nc, a, sem, psum, ps_s, locals())
        block_b(nc, a, out, sem, psum, ps_s, locals())


def block_a(nc, a, sem, psum, ps_s, m):
    quad_mask, row_mask, iota8, out_bias, gate_bias, g2, be2 = (
        m[n] for n in ("quad_mask", "row_mask", "iota8", "out_bias", "gate_bias", "g2", "be2"))
    sel_bf, ident_bf = m["sel_bf"], m["ident_bf"]
    held = m["held"]
    ident, dram_q, k_all, src_all = m["ident"], m["dram_q"], m["k_all"], m["src_all"]
    w1_hi, w1_lo, proj_t, vec = m["w1_hi"], m["w1_lo"], m["proj_t"], m["vec"]
    w2_hi, w2_lo = m["w2_hi"], m["w2_lo"]
    q_bias, neg_half, dram_res = m["q_bias"], m["neg_half"], m["dram_res"]
    f0, f1, f2, r0 = psum
    with ExitStack() as ctx:
        def sb(name, shape, dt=F32):
            return ctx.enter_context(nc.sbuf_tensor(name, shape, dt))

        x_all = sb("x_all", [P, S, D])
        c_all = sb("c_all", [P, S, D])
        rope = sb("rope", [P, 4, T])
        vec_rows = sb("vec_rows", [P, P])
        proj_rows = sb("proj_rows", [P, 4, P])
        wq_raw = sb("wq_raw", [P, NH, HD])
        kv_raw = sb("kv_raw", [P, 2, HD])
        wo_x = sb("wo_x", [P, D])
        rms1 = sb("rms1", [P, 1])
        wq = sb("wq", [P, NH, HD])
        wq_sw = wq_raw[:, :, :].rearrange("p n (two h) -> p n two h", two=2)
        wk = sb("wk", [P, NH, HD])
        wk_sw = vec_rows[:, :].rearrange("p (n two h) -> p n two h", n=NH, two=2)
        wv = sb("wv", [P, HD])
        mask_u8 = sb("mask_u8", [P, S * T], U8)
        mask_g = sb("mask_g", [P, 2, TOK], BF16)
        ones_bf = sb("ones_bf", [P, P], BF16)
        stats = sb("stats", [P, 8, 6])
        mv = sb("mv", [P, 8, 2])
        msq = sb("msq", [P, 4])
        var_in = sb("var_in", [P, 8])
        rstd_in = sb("rstd_in", [P, 8])
        xn = sb("xn", [P, GB, D])
        mn = sb("mn", [P, GB, D])
        xn_t = sb("xn_t", [P, TOK])
        mn_t = sb("mn_t", [P, TOK])
        q_cos = sb("q_cos", [P, TOK])
        q_sin = sb("q_sin", [P, TOK])
        k_cos = sb("k_cos", [P, TOK])
        k_sin = sb("k_sin", [P, TOK])
        q_r = sb("q_r", [P, 2, GB, T])
        k_r = sb("k_r", [P, 2, GB, T])
        v_tok = sb("v_tok", [P, 2, GB, HD])
        neg_max = sb("neg_max", [P, NH, GB])
        row_sum = sb("row_sum", [P, NH, GB])
        row_rec = sb("row_rec", [P, NH, GB])
        both = sb("probs_both", [P, 2, NH, GB, T])
        probs, probs_t = both[:, 0], both[:, 1]
        q_out = sb("q_out", [P, 2, GB, T])
        enc_t = sb("enc_t", [P, TOK])
        x1 = sb("x1", [P, 2, GB, 2, D])
        sel_f = x1[0:3 * E, 1].rearrange("p b two d -> p (b two) d")
        stats1 = sb("stats1", [P, GB, 6])
        mv1 = sb("mv1", [P, GB, 2])
        var1 = sb("var1", [P, GB])
        rstd1 = sb("rstd1", [P, GB])
        src_t = proj_rows[:, :, :].rearrange("p c d -> p (c d)")

        ld_x = [sem(f"ld_x{i}") for i in range(2)]
        ld_k = sem("ld_k")
        ld_w = [sem(f"ld_w{i}") for i in range(5)]
        vec_ps, vec_sb = sem("vec_ps"), sem("vec_sb")
        small_w = sem("small_w")
        small_a = sem("small_a")
        w_ps, w_hi_sb, w_lo_sb = sem("w_ps"), sem("w_hi_sb"), sem("w_lo_sb")
        in_stats, in_mv, in_var, in_rstd = sem("in_stats"), sem("in_mv"), sem("in_var"), sem("in_rstd")
        xn_sb, mn_sb = sem("xn_sb"), sem("mn_sb")
        xt_ps, mt_ps, xt_sb, mt_sb = sem("xt_ps"), sem("mt_ps"), sem("xt_sb"), sem("mt_sb")
        fq_ps, fqs_ps, fk_ps, fks_ps, fv_ps = (sem(n) for n in ("fq_ps", "fqs_ps", "fk_ps", "fks_ps", "fv_ps"))
        mask_rdy = sem("mask_rdy")
        rq, rk = sem("rq"), sem("rk")
        q_rdy, k_rdy, v_sb = sem("q_rdy"), sem("k_rdy"), sem("v_sb")
        sc_ps, max_sb, exp_sb, rec_sb = (sem(n) for n in ("sc_ps", "max_sb", "exp_sb", "rec_sb"))
        prob_sb = [sem("prob_pool"), sem("prob_dve")]
        pt_ps, pt_sb = sem("pt_ps"), sem("pt_sb")
        enc_ps, enc_sb, op_ps, x1_sb = sem("enc_ps"), sem("enc_sb"), sem("op_ps"), sem("x1_sb")
        st1, mv1_s, var1_s, rstd1_s, src_sb = (sem(n) for n in ("st1", "mv1_s", "var1_s", "rstd1_s", "src_sb"))
        stored = [sem(f"stored{i}") for i in range(2)]
        q_stored = [sem(f"q_stored{i}") for i in range(2)]
        srct_ps, srct_sb, bq_ps, bq_sb, bk_ps, bk_sb = (
            sem(n) for n in ("srct_ps", "srct_sb", "bq_ps", "bq_sb", "bk_ps", "bk_sb"))

        w1_rows = both[:, :, :, :, :].rearrange("p a h b t -> p (a h b) t")
        w2_rows = k_all[:, :, :].rearrange("p a b -> p (a b)").rearrange("p (e f) -> p e f", e=E)
        q_g = dram_q.rearrange("(g b) p t -> g p b t", b=GB)
        res_g = dram_res.rearrange("(g b) t two d -> g t b two d", b=GB)
        x_g = a["x"].rearrange("(g b) t d -> g t b d", b=GB)
        c_g = a["ctx"].rearrange("(g b) t d -> g t b d", b=GB)

        def seqs(tile, g):
            return tile[:, bass.ts(g, GB), :]

        def ts_of(tile, g):
            return tile[:, :, bass.ts(g, GB)].rearrange("p t s -> p s t")

        block = ctx.enter_context(nc.Block())

        @block.sync
        def _(sp):
            def load(g):
                sp.dma_start(seqs(x_all, g), x_g[g]).then_inc(ld_x[g % 2], 16)
                sp.dma_start(seqs(c_all, g), c_g[g]).then_inc(ld_x[g % 2], 16)

            load(0)
            sp.dma_start(ident[:, :], a["ident"]).then_inc(ld_w[0], 16)
            for row, n, src in ((V_B1, 32, a["b1"].rearrange("e (c f) -> (e c) f", c=FC)), (V_B2, E, a["b2"]),
                                (V_INB, 3, a["in_b"].rearrange("(c f) -> c f", c=3)),
                                (V_G1, 1, a["ln1_g"].rearrange("(a f) -> a f", a=1)),
                                (V_BE1, 1, a["ln1_b"].rearrange("(a f) -> a f", a=1)),
                                (V_RMS, 1, a["rms"].rearrange("(a f) -> a f", a=1)), (V_GATE, E, a["gate_w"])):
                sp.dma_start(vec_rows[row:row + n, :], src).then_inc(ld_w[0], 16)
            for g in range(1, NG):
                if g >= 2:
                    sp.wait_ge(ld_x[g % 2], g // 2 * 32)
                load(g)
            consts = [(quad_mask[:, :], a["quad_mask"]), (row_mask[:, :], a["row_mask"]),
                      (iota8[:, :, :], a["iota8"]),
                      (out_bias[:, :], a["out_b"].unsqueeze(0).to_broadcast([P, D])),
                      (gate_bias[:, :], a["gate_b"].unsqueeze(0).to_broadcast([P, E])),
                      (g2[:, :], a["ln2_g"].unsqueeze(0).to_broadcast([P, D])),
                      (be2[:, :], a["ln2_b"].unsqueeze(0).to_broadcast([P, D]))]
            assert len(consts) == 7
            for dst, src in consts:
                sp.dma_start(dst, src).then_inc(ld_k, 16)

            def step(g, p, first, last):
                sp.wait_ge(src_sb, g * GB + GB)
                sp.dma_start(res_g[g], x1[:, p]).then_inc(stored[p], 16)
                sp.wait_ge(bq_sb, g + 1)
                sp.dma_start(q_g[g], q_out[:, p]).then_inc(q_stored[p], 16)

            run_steps(sp, NG, step)
            for p in range(2):
                sp.wait_ge(stored[p], 16 + 16 * NG // 2)
                sp.wait_ge(q_stored[p], 16 + 16 * NG // 2)
            sp.wait_ge(ld_k, 16 * 7)

        @block.scalar
        def _(act):
            act.dma_start(proj_rows[:, 0:3, :], a["in_w"].rearrange("(c j) d -> j c d", c=3)).then_inc(ld_w[1], 16)
            act.dma_start(proj_rows[:, 3, :], a["out_w"]).then_inc(ld_w[1], 16)
            act.dma_start(wq_raw[:, :, :], a["q_w"].rearrange("n d h -> d n h")).then_inc(ld_w[1], 16)
            act.dma_start(kv_raw[:, :, :], a["kv_w"].rearrange("c k d h -> d (c k) h")).then_inc(ld_w[1], 16)
            act.dma_start(wo_x[:, :], a["wo_x"].rearrange("n h d -> (n h) d")).then_inc(ld_w[1], 16)
            act.dma_start(rope[:, :, :], a["rope"].rearrange("n p t -> p n t")).then_inc(ld_w[2], 16)
            act.dma_start(sel_f[:, :, :], a["expert_sel"]).then_inc(ld_w[2], 16)
            act.dma_start(mask_u8[:, :], a["mask"].rearrange("s t -> (s t)").unsqueeze(0).to_broadcast([P, S * T])
                          ).then_inc(ld_w[2], 16)
            act.wait_ge(ld_w[0], 16 * 8)
            act.dma_start(w1_rows, a["w1"].rearrange("e (c f) d -> f (e c) d", c=FC)).then_inc(ld_w[3], 16)
            act.dma_start(w2_rows, a["w2"].rearrange("e d f -> d e f")).then_inc(ld_w[4], 16)
            act.wait_ge(vec_ps, 1)
            nc.scalar.activation(vec[:, :], r0[:, 0:V_ROWS], ACT.Copy).then_inc(vec_sb, 1)
            act.wait_ge(vec_ps, 2)
            nc.scalar.activation(proj_t[:, :, :], f0[:, :], ACT.Copy).then_inc(vec_sb, 1)

            def norm_ctx(g):
                act.wait_ge(in_rstd, g + 1)
                if not isinstance(g, int) or g > 0:
                    act.wait_ge(mt_ps, g)
                for b in range(GB):
                    nc.scalar.activation(mn[:, b, :], c_all[:, g * GB + b, :], ACT.Copy,
                                         scale=rstd_in[:, GB + b:GB + b + 1]).then_inc(mn_sb, 1)

            def evac_front(g):
                act.wait_ge(xt_ps, g + 1)
                if not isinstance(g, int) or g > 0:
                    act.wait_ge(fqs_ps, g)
                nc.scalar.activation(xn_t[:, :], f0[:, :], ACT.Copy).then_inc(xt_sb, 1)
                act.wait_ge(mt_ps, g + 1)
                if not isinstance(g, int) or g > 0:
                    act.wait_ge(fv_ps, g)
                nc.scalar.activation(mn_t[:, :], f1[:, :], ACT.Copy).then_inc(mt_sb, 1)

            def evac_v(g, p):
                act.wait_ge(fv_ps, g + 1)
                if not isinstance(g, int) or g > 1:
                    act.wait_ge(enc_ps, g - 1)
                nc.scalar.activation(v_tok[:, p, :, :], f0[:, 0:GB * HD], ACT.Copy).then_inc(v_sb, 1)

            def evac_src(g):
                act.wait_ge(srct_ps, g + 1)
                nc.scalar.activation(src_t[:, :], r0[:, :], ACT.Copy).then_inc(srct_sb, 1)

            def keep_src(g):
                act.wait_ge(srct_sb, g * 2 + 1)
                nc.scalar.activation(ts_of(src_all, g), src_t[:, :].rearrange("p (s t) -> p s t", s=GB), ACT.Copy
                                     ).then_inc(srct_sb, 1)

            def evac_bq(g, p):
                act.wait_ge(bq_ps, g + 1)
                act.wait_ge(small_w, 7)
                act.wait_ge(q_stored[p], g * 8 + (16 - 8 * p))
                nc.scalar.activation(q_out[:, p, :, :], r0[:, :].rearrange("p (s t) -> p s t", s=GB), ACT.Identity,
                                     bias=q_bias[:, 0:1], scale=FD ** -0.5).then_inc(bq_sb, 1)

            def exps(g, h, first):
                act.wait_ge(max_sb, g * NH + h + 1)
                if not first:
                    act.wait_ge(pt_ps, g * NH - NH + h + 1)
                    act.wait_ge(rec_sb, g * NH - NH + h + 1)
                for b in range(GB):
                    nc.scalar.activation(probs[:, h, b, :], ps_s[:, h, b * T:(b + 1) * T], ACT.Exp,
                                         bias=neg_max[:, h, b:b + 1], accum_out=row_sum[:, h, b:b + 1]
                                         ).then_inc(exp_sb, 1)

            def evac_probs(g, h, first):
                act.wait_ge(pt_ps, g * NH + h + 1)
                if not first:
                    act.wait_ge(enc_ps, g)
                nc.scalar.activation(probs_t[:, h, :, :], ps_s[:, h, :], ACT.Copy).then_inc(pt_sb, 1)

            def evac_enc(g):
                act.wait_ge(enc_ps, g + 1)
                nc.scalar.activation(enc_t[:, :], r0[:, :], ACT.Copy).then_inc(enc_sb, 1)

            def evac_bk(g):
                act.wait_ge(bk_ps, g + 1)
                nc.scalar.activation(ts_of(k_all, g), r0[:, :].rearrange("p (s t) -> p s t", s=GB), ACT.Identity,
                                     bias=vec[:, V_INB + 1:V_INB + 2]).then_inc(bk_sb, 1)

            norm_ctx(0)
            evac_front(0)
            evac_v(0, 0)
            for n in range(16):
                act.wait_ge(w_ps, n + 1)
                dst = w1_hi[:, n * TOK:(n + 1) * TOK] if n < 8 else w2_hi[:, n - 8, :, :]
                nc.scalar.activation(dst, ps_s[:, n % 4, :], ACT.Copy).then_inc(w_hi_sb, 1)

            def step(g, p, first, last):
                if not last:
                    norm_ctx(g + 1)
                if not first:
                    evac_enc(g - 1)
                if not last:
                    evac_front(g + 1)
                for h in range(NH):
                    exps(g, h, first)
                evac_probs(g, 0, first)
                if not first:
                    evac_src(g - 1)
                evac_probs(g, 1, first)
                if not last:
                    evac_v(g + 1, 1 - p)
                evac_probs(g, 2, first)
                if not first:
                    keep_src(g - 1)
                    evac_bq(g - 1, 1 - p)
                evac_probs(g, 3, first)
                if not first:
                    evac_bk(g - 1)

            run_steps(act, NG, step)
            evac_enc(NG - 1)
            evac_src(NG - 1)
            keep_src(NG - 1)
            evac_bq(NG - 1, (NG - 1) % 2)
            evac_bk(NG - 1)

        @block.vector
        def _(dve):
            nc.vector.memset(ones_bf[:, :], 1.0).then_inc(small_w, 1)
            nc.vector.memset(neg_half[:, :], -0.5).then_inc(small_w, 1)
            for p in range(2):
                nc.vector.memset(held[:, 5 + p:6 + p], 0.0).then_inc(stored[p], 16)
                nc.vector.memset(held[:, 8 + p:9 + p], 0.0).then_inc(q_stored[p], 16)
            nc.vector.memset(held[:, 7:8], 0.0).then_inc(bk_sb, 1)
            def hold(cell):
                nc.vector.memset(held[:, cell:cell + 1], 0.0)

            def stats_in(g, p):
                dve.wait_ge(ld_x[p], g * 16 + (32 - 16 * p))
                if not isinstance(g, int) or g > 0:
                    dve.wait_ge(in_mv, g * 8)
                for b in range(GB):
                    nc.vector.bn_stats(stats[:, b, :], x_all[:, g * GB + b, :]).then_inc(in_stats, 1)
                    nc.vector.bn_stats(stats[:, GB + b, :], c_all[:, g * GB + b, :]).then_inc(in_stats, 1)
                if not isinstance(g, int) or g > 0:
                    dve.wait_ge(in_var, g * 3)
                    dve.wait_ge(xn_sb, g * GB)
                dve.wait_ge(in_stats, g * 8 + 8)
                hold(0)
                for b in range(2 * GB):
                    nc.vector.bn_aggr(mv[:, b, :], stats[:, b, :]).then_inc(in_mv, 1)
                dve.wait_ge(in_mv, g * 8 + 8)
                if not isinstance(g, int) or g > 0:
                    dve.wait_ge(in_rstd, g)
                nc.vector.tensor_scalar(var_in[:, 0:GB], mv[:, 0:GB, 1], 1.0 + EPS_RMS, EPS_RMS * EPS_LN,
                                        ALU.mult, ALU.add).then_inc(in_var, 1)
                nc.vector.tensor_tensor(msq[:, :], mv[:, GB:, 0], mv[:, GB:, 0], ALU.mult).then_inc(in_var, 1)
                dve.wait_ge(in_var, g * 3 + 2)
                nc.vector.scalar_tensor_tensor(var_in[:, GB:], msq[:, :], EPS_RMS, mv[:, GB:, 1], ALU.add, ALU.add
                                               ).then_inc(in_var, 1)

            def norm_x(g):
                dve.wait_ge(in_rstd, g + 1)
                if not isinstance(g, int) or g > 0:
                    dve.wait_ge(xt_ps, g)
                for b in range(GB):
                    nc.vector.tensor_scalar(xn[:, b, :], x_all[:, g * GB + b, :], mv[:, b, 0:1], rstd_in[:, b:b + 1],
                                            ALU.subtract, ALU.mult).then_inc(xn_sb, 1)

            def table(n):
                return rope[:, n:n + 1, :].to_broadcast([P, GB, T])

            def cols(t):
                return t[:, :].rearrange("p (s t) -> p s t", s=GB)

            products = (
                (fq_ps, q_cos, f2, table(0), rq), (fqs_ps, q_sin, f0, table(1), rq),
                (fk_ps, k_cos, f1, table(2), rk), (fks_ps, k_sin, f2, table(3), rk))

            def rotate(g, n):
                done, dst, bank, table, product = products[n]
                if not isinstance(g, int) or g > 0:
                    dve.wait_ge(q_rdy if n < 2 else k_rdy, g)
                dve.wait_ge(done, g + 1)
                nc.vector.tensor_tensor(cols(dst), cols(bank), table, ALU.mult).then_inc(product, 1)

            def mask_of(g, p):
                nc.vector.tensor_scalar(mask_g[:, p, :], mask_u8[:, bass.ts(g, TOK)], FILL, -FILL, ALU.mult, ALU.add
                                        ).then_inc(mask_rdy, 1)

            def maximum(g, h, first):
                dve.wait_ge(sc_ps, g * NH + h + 1)
                if not first:
                    dve.wait_ge(exp_sb, g * 16 - 16 + 4 * h + 4)
                nc.vector.tensor_reduce(neg_max[:, h, :], ps_s[:, h, :].rearrange("p (s t) -> p s t", s=GB),
                                        AX_X, ALU.max, negate=True).then_inc(max_sb, 1)

            def normalise(g, h, first):
                dve.wait_ge(exp_sb, g * 16 + 4 * h + 4)
                if not first:
                    dve.wait_ge(prob_sb[h % 2], g * 2 - 2 + h // 2 + 1)
                nc.vector.reciprocal(row_rec[:, h, :], row_sum[:, h, :]).then_inc(rec_sb, 1)
                if h % 2 == 0:
                    return
                dve.wait_ge(rec_sb, g * NH + h + 1)
                nc.vector.tensor_tensor(probs[:, h, :, :], probs[:, h, :, :],
                                        row_rec[:, h, :].unsqueeze(2).to_broadcast([P, GB, T]), ALU.mult
                                        ).then_inc(prob_sb[1], 1)

            def residual(g, p):
                dve.wait_ge(op_ps, g + 1)
                dve.wait_ge(stored[p], g * 8 + (16 - 8 * p))
                nc.vector.tensor_tensor(x1[:, p, :, 0, :], r0[:, :].rearrange("p (s d) -> p s d", s=GB),
                                        seqs(x_all, g), ALU.add).then_inc(x1_sb, 1)
                dve.wait_ge(x1_sb, g + 1)
                for b in range(GB):
                    nc.vector.bn_stats(stats1[:, b, :], x1[:, p, b, 0, :]).then_inc(st1, 1)
                dve.wait_ge(st1, g * GB + GB)
                hold(1)
                for b in range(GB):
                    nc.vector.bn_aggr(mv1[:, b, :], stats1[:, b, :]).then_inc(mv1_s, 1)
                dve.wait_ge(mv1_s, g * GB + GB)
                nc.vector.tensor_scalar(var1[:, :], mv1[:, :, 1], EPS_LN, None, ALU.add).then_inc(var1_s, 1)

            def normed(g, p):
                dve.wait_ge(rstd1_s, g + 1)
                for b in range(GB):
                    nc.vector.tensor_scalar(x1[:, p, b, 1, :], x1[:, p, b, 0, :], mv1[:, b, 0:1], rstd1[:, b:b + 1],
                                            ALU.subtract, ALU.mult).then_inc(src_sb, 1)

            stats_in(0, 0)
            norm_x(0)
            dve.wait_ge(vec_sb, 1)
            dve.wait_ge(ld_w[1], 80)
            dve.wait_ge(ld_w[2], 48)
            nc.vector.tensor_scalar(rms1[:, :], vec[:, V_RMS:V_RMS + 1], 1.0, None, ALU.add).then_inc(small_w, 1)
            dve.wait_ge(small_w, 3)
            nc.vector.tensor_scalar(wq[:, :, :], wq_raw[:, :, :], rms1[:, 0:1], HD ** -0.5, ALU.mult, ALU.mult
                                    ).then_inc(small_w, 1)
            nc.vector.tensor_scalar(wk[:, :, :], kv_raw[:, 0:1, :].to_broadcast([P, NH, HD]), rms1[:, 0:1], None,
                                    ALU.mult).then_inc(small_w, 1)
            nc.vector.tensor_scalar(wv[:, :], kv_raw[:, 1, :], rms1[:, 0:1], None, ALU.mult).then_inc(small_w, 1)
            nc.vector.tensor_scalar(q_bias[:, :], vec[:, V_INB:V_INB + 1], FD ** -0.5, None, ALU.mult
                                    ).then_inc(small_w, 1)
            dve.wait_ge(small_w, 5)
            for half in range(2):
                for dst, src in ((wq_sw, wq), (wk_sw, wk)):
                    o = (1 - half) * (HD // 2)
                    nc.vector.tensor_copy(dst[:, :, half, :], src[:, :, o:o + HD // 2]).then_inc(small_w, 1)
            mask_of(0, 0)
            for n in range(4):
                rotate(0, n)
            for n in range(16):
                dve.wait_ge(w_hi_sb, n + 1)
                span = slice(n * TOK, (n + 1) * TOK)
                hi = w1_hi[:, span] if n < 8 else w2_hi[:, n - 8, :, :].rearrange("p c d -> p (c d)")
                lo = w1_lo[:, span] if n < 8 else w2_lo[:, n - 8, :, :].rearrange("p c d -> p (c d)")
                nc.vector.tensor_tensor(lo, ps_s[:, n % 4, :], hi.bitcast(F32), ALU.subtract).then_inc(w_lo_sb, 1)

            def step(g, p, first, last):
                if not last:
                    mask_of(g + 1, 1 - p)
                    stats_in(g + 1, 1 - p)
                if not last:
                    norm_x(g + 1)
                maximum(g, 0, first)
                maximum(g, 1, first)
                if not first:
                    residual(g - 1, 1 - p)
                if not last:
                    rotate(g + 1, 0)
                normalise(g, 0, first)
                maximum(g, 2, first)
                if not last:
                    rotate(g + 1, 1)
                normalise(g, 1, first)
                maximum(g, 3, first)
                if not first:
                    normed(g - 1, 1 - p)
                normalise(g, 2, first)
                if not last:
                    rotate(g + 1, 2)
                    rotate(g + 1, 3)
                normalise(g, 3, first)

            run_steps(dve, NG, step)
            residual(NG - 1, (NG - 1) % 2)
            normed(NG - 1, (NG - 1) % 2)

        @block.gpsimd
        def _(pool):
            def rstd_of_inputs(g):
                pool.wait_ge(in_var, g * 3 + 3)
                if not isinstance(g, int) or g > 0:
                    pool.wait_ge(xn_sb, g * GB)
                    pool.wait_ge(mn_sb, g * GB)
                nc.gpsimd.tensor_tensor(rstd_in[:, :], var_in[:, :], neg_half[:, :], ALU.pow).then_inc(in_rstd, 1)

            def rotated(g, p):
                pool.wait_ge(rq, g * 2 + 2)
                if not isinstance(g, int) or g > 1:
                    pool.wait_ge(sc_ps, g * NH - NH)
                nc.gpsimd.tensor_tensor(q_r[:, p, :, :], q_cos[:, :].rearrange("p (s t) -> p s t", s=GB),
                                        q_sin[:, :].rearrange("p (s t) -> p s t", s=GB), ALU.add).then_inc(q_rdy, 1)
                pool.wait_ge(rk, g * 2 + 2)
                nc.gpsimd.tensor_tensor(k_r[:, p, :, :], k_cos[:, :].rearrange("p (s t) -> p s t", s=GB),
                                        k_sin[:, :].rearrange("p (s t) -> p s t", s=GB), ALU.add).then_inc(k_rdy, 1)

            def normalise(g, h):
                pool.wait_ge(rec_sb, g * NH + h + 1)
                nc.gpsimd.tensor_tensor(probs[:, h, :, :], probs[:, h, :, :],
                                        row_rec[:, h, :].unsqueeze(2).to_broadcast([P, GB, T]), ALU.mult
                                        ).then_inc(prob_sb[0], 1)

            def rstd_1(g):
                pool.wait_ge(var1_s, g + 1)
                nc.gpsimd.tensor_tensor(rstd1[:, :], var1[:, :], neg_half[:, 0:GB], ALU.pow).then_inc(rstd1_s, 1)

            pool.wait_ge(small_w, 2)
            rstd_of_inputs(0)
            rotated(0, 0)
            pool.wait_ge(ld_w[0], 16 * 8)
            pool.wait_ge(ld_w[2], 48)
            nc.gpsimd.tensor_copy(ident_bf[:, :], ident[:, :])
            nc.gpsimd.tensor_copy(sel_bf[:, :, :], sel_f[:, :, :])

            def step(g, p, first, last):
                if not last:
                    rstd_of_inputs(g + 1)
                normalise(g, 0)
                if not first:
                    rstd_1(g - 1)
                normalise(g, 2)
                if not last:
                    rotated(g + 1, 1 - p)

            run_steps(pool, NG, step)
            rstd_1(NG - 1)

        @block.tensor
        def _(pe):
            pe.wait_ge(ld_w[0], 16 * 8)
            nc.tensor.transpose(r0[:, 0:V_ROWS], vec_rows[0:V_ROWS, :], ident[0:V_ROWS, 0:V_ROWS]).then_inc(vec_ps, 1)
            pe.wait_ge(ld_w[1], 80)
            for n in range(4):
                mm = nc.tensor.transpose(f0[:, n * P:(n + 1) * P], proj_rows[:, n, :], ident[:, :])
            mm.then_inc(vec_ps, 1)

            def front_transposes(g):
                pe.wait_ge(xn_sb, g * GB + GB)
                if not isinstance(g, int) or g > 0:
                    pe.wait_ge(v_sb, g)
                else:
                    pe.wait_ge(vec_sb, 2)
                for b in range(GB):
                    mm = nc.tensor.transpose(f0[:, b * P:(b + 1) * P], xn[:, b, :], ident[:, :])
                mm.then_inc(xt_ps, 1)
                pe.wait_ge(mn_sb, g * GB + GB)
                if not isinstance(g, int) or g > 0:
                    pe.wait_ge(rk, g * 2)
                for b in range(GB):
                    mm = nc.tensor.transpose(f1[:, b * P:(b + 1) * P], mn[:, b, :], ident[:, :])
                mm.then_inc(mt_ps, 1)

            def front_q(g):
                if isinstance(g, int) and g == 0:
                    pe.wait_ge(small_w, 11)
                pe.wait_ge(xt_sb, g + 1)
                nc.tensor.matmul(f2[:, :], wq[:, :, :], xn_t[:, :], start=True, stop=True).then_inc(fq_ps, 1)
                nc.tensor.matmul(f0[:, :], wq_sw[:, :, :, :], xn_t[:, :], start=True, stop=True).then_inc(fqs_ps, 1)

            def front_k(g):
                pe.wait_ge(mt_sb, g + 1)
                nc.tensor.matmul(f1[:, :], wk[:, :, :], mn_t[:, :], start=True, stop=True).then_inc(fk_ps, 1)

            def front_k_exchanged(g):
                pe.wait_ge(rq, g * 2 + 1)
                nc.tensor.matmul(f2[:, :], wk_sw[:, :, :, :], mn_t[:, :], start=True, stop=True).then_inc(fks_ps, 1)

            def front_v(g):
                pe.wait_ge(rq, g * 2 + 2)
                for b in range(GB):
                    mm = nc.tensor.matmul(f0[:, b * HD:(b + 1) * HD], mn_t[:, b * T:(b + 1) * T], wv[:, :],
                                          start=True, stop=True)
                mm.then_inc(fv_ps, 1)

            def back_transposes(g, p):
                pe.wait_ge(src_sb, g * GB + GB)
                for b in range(GB):
                    mm = nc.tensor.transpose(r0[:, b * P:(b + 1) * P], x1[:, p, b, 1, :], ident[:, :])
                mm.then_inc(srct_ps, 1)

            def back_q(g):
                pe.wait_ge(srct_sb, g * 2 + 1)
                nc.tensor.matmul(r0[:, :], proj_t[:, 0, :], src_t[:, :], start=True, stop=True).then_inc(bq_ps, 1)

            def back_k(g):
                pe.wait_ge(bq_sb, g + 1)
                nc.tensor.matmul(r0[:, :], proj_t[:, 1, :], src_t[:, :], start=True, stop=True).then_inc(bk_ps, 1)

            def scores(g, h, p, first):
                if h == 0:
                    pe.wait_ge(mask_rdy, g + 1)
                    pe.wait_ge(q_rdy, g + 1)
                    pe.wait_ge(k_rdy, g + 1)
                    if first:
                        pe.wait_ge(w_hi_sb, 16)
                        pe.wait_ge(w_lo_sb, 16)
                if not first:
                    pe.wait_ge(pt_sb, g * NH - NH + h + 1)
                rows = slice(h * HD, (h + 1) * HD)
                for b in range(GB):
                    cols = slice(b * T, (b + 1) * T)
                    nc.tensor.matmul(ps_s[:, h, cols], ones_bf[h * HD:h * HD + 1, :],
                                     mask_g[h * HD:h * HD + 1, p, cols], start=True, stop=False)
                    mm = nc.tensor.matmul(ps_s[:, h, cols], q_r[rows, p, b, :], k_r[rows, p, b, :],
                                          start=False, stop=True)
                mm.then_inc(sc_ps, 1)

            def turn_probs(g, h):
                pe.wait_ge(prob_sb[h % 2], g * 2 + h // 2 + 1)
                for b in range(GB):
                    mm = nc.tensor.transpose(ps_s[:, h, b * T:(b + 1) * T], probs[:, h, b, :], ident[:, :])
                mm.then_inc(pt_ps, 1)

            def attend(g, p):
                pe.wait_ge(pt_sb, g * NH + NH)
                pe.wait_ge(v_sb, g + 1)
                pe.wait_ge(bk_sb, g + 1)
                for b in range(GB):
                    for h in range(NH):
                        mm = nc.tensor.matmul(r0[h * HD:(h + 1) * HD, b * T:(b + 1) * T], v_tok[:, p, b, :],
                                              probs_t[:, h, b, :], start=True, stop=True)
                mm.then_inc(enc_ps, 1)

            def out_proj(g):
                pe.wait_ge(enc_sb, g + 1)
                for b in range(GB):
                    mm = nc.tensor.matmul(r0[:, b * D:(b + 1) * D], enc_t[:, b * T:(b + 1) * T], wo_x[:, :],
                                          start=True, stop=True)
                mm.then_inc(op_ps, 1)

            front_transposes(0)
            front_q(0)
            front_k(0)
            front_k_exchanged(0)
            front_v(0)
            for n in range(16):
                if n == 0:
                    pe.wait_ge(ld_w[3], 16)
                if n == 8:
                    pe.wait_ge(ld_w[4], 16)
                if n >= 4:
                    pe.wait_ge(w_hi_sb, n - 3)
                    pe.wait_ge(w_lo_sb, n - 3)
                for c in range(FC):
                    src = w1_rows[:, n * FC + c, :] if n < 8 else w2_rows[:, n - 8, c * P:(c + 1) * P]
                    mm = nc.tensor.transpose(ps_s[:, n % 4, c * P:(c + 1) * P], src, ident[:, :])
                mm.then_inc(w_ps, 1)

            def step(g, p, first, last):
                scores(g, 0, p, first)
                if not first:
                    attend(g - 1, 1 - p)
                scores(g, 1, p, first)
                if not last:
                    front_transposes(g + 1)
                if not first:
                    out_proj(g - 1)
                if not last:
                    front_q(g + 1)
                scores(g, 2, p, first)
                if not last:
                    front_k(g + 1)
                scores(g, 3, p, first)
                if not last:
                    front_k_exchanged(g + 1)
                turn_probs(g, 0)
                turn_probs(g, 1)
                if not first:
                    back_transposes(g - 1, 1 - p)
                if not last:
                    front_v(g + 1)
                turn_probs(g, 2)
                if not first:
                    back_q(g - 1)
                turn_probs(g, 3)
                if not first:
                    back_k(g - 1)

            run_steps(pe, NG, step)
            attend(NG - 1, (NG - 1) % 2)
            out_proj(NG - 1)
            back_transposes(NG - 1, (NG - 1) % 2)
            back_q(NG - 1)
            back_k(NG - 1)


def block_b(nc, a, out, sem, psum, ps_s, m):
    quad_mask, row_mask, iota8, out_bias, gate_bias, g2, be2 = (
        m[n] for n in ("quad_mask", "row_mask", "iota8", "out_bias", "gate_bias", "g2", "be2"))
    sel_bf, ident_bf = m["sel_bf"], m["ident_bf"]
    held = m["held"]
    ident, dram_q, k_all, src_all = m["ident"], m["dram_q"], m["k_all"], m["src_all"]
    w1_hi, w1_lo, proj_t, vec = m["w1_hi"], m["w1_lo"], m["proj_t"], m["vec"]
    w2_hi, w2_lo = m["w2_hi"], m["w2_lo"]
    neg_half, dram_res = m["neg_half"], m["dram_res"]
    h_ps = psum[0:2]
    y_ps, a_ps = psum[2], psum[3]
    with ExitStack() as ctx:
        def sb(name, shape, dt=F32):
            return ctx.enter_context(nc.sbuf_tensor(name, shape, dt))

        q_c = sb("q_c", [P, 2, S, CT])
        s_c = sb("s_c", [P, CT, 4, S])
        k_bd = sb("k_bd", [P, CT, QUAD, S])
        v_bd = sb("v_bd", [P, CT, FH // QUAD, QUAD, FD])
        res = sb("res", [P, 2, NQ, 2, D])
        neg_max = sb("neg_max2", [P, 4, 16])
        row_sum = sb("row_sum2", [P, 4, 16])
        row_rec = sb("row_rec2", [P, 4, 16])
        ex = sb("ex", [P, 4, TOK])
        ex_t = s_c[:, :, :, :].rearrange("p t j s -> p (t j s)").rearrange("p (g n) -> p g n", g=4)
        where_keys = k_bd[:, :, :, :].rearrange("p t h s -> p (t h s)").rearrange("p (i n) -> p i n", i=4)
        ctx_tok = where_keys[:, 0, :].rearrange("p (q d) -> p q d", q=NQ)
        ctx_t = where_keys[:, 1, :]
        y_hat = where_keys[:, 2, :].rearrange("p (q d) -> p q d", q=NQ)
        o_hat = where_keys[:, 3, :].rearrange("p (q d) -> p q d", q=NQ)
        stats = sb("stats2", [P, NQ, 6])
        mv = sb("mv2", [P, NQ, 2])
        var = sb("var2", [P, NQ])
        rstd = sb("rstd2", [P, NQ])
        tok_t = sb("tok_t", [P, 2, TOK])
        tok_hi = sb("tok_hi", [P, 2, TOK], F32R)
        tok_lo = sb("tok_lo", [P, 2, TOK], F32R)
        logit = sb("logit", [P, NQ, E])
        top = sb("top", [P, NQ, 8])
        top_i = sb("top_i", [P, NQ, 8], U32)
        top_f = sb("top_f", [P, NQ, 2])
        gap = sb("gap", [P, NQ])
        gap_e = sb("gap_e", [P, NQ])
        wt_den = sb("wt_den", [P, NQ])
        wt = sb("wt", [P, NQ, 2])
        pick = sb("pick", [P, 2, NQ, E])
        comb = sb("comb", [P, NQ, E])
        part_bf = sb("part_bf", [P, NQ, 3, E], BF16)
        rest = sb("rest", [P, 2, NQ, E])
        comb_t = sb("comb_t", [3 * E, 2, TOK], BF16)
        comb_b = sb("comb_b", [P, 2, TOK])
        hid_hi = sb("hid_hi", [P, 2, FC, TOK], F32R)
        hid_x = sb("hid_x", [P, FC, TOK])
        hid_lo = sb("hid_lo", [P, FC, TOK], F32R)
        term = sb("term", [P, 2, TOK])
        acc = sb("acc", [P, 2, TOK])
        stats3 = sb("stats3", [P, NQ, 6])
        mv3 = sb("mv3", [P, NQ, 2])
        var3 = sb("var3", [P, NQ])
        rstd3 = sb("rstd3", [P, NQ])

        ld_q = [sem(f"ld_q{i}") for i in range(2)]
        ld_r = [sem(f"ld_r{i}") for i in range(2)]
        s_rdy = sem("s_rdy")
        kbd_rdy, v_ps, v_rdy = sem("kbd_rdy"), sem("v_ps"), sem("v_rdy")
        sc_ps, mx_sb, sub_sb, ex_sb, sum_sb, rec_sb = (sem("b_" + n) for n in ("sc", "mx", "sub", "ex", "sum", "rec"))
        pt_ps, pt_act, pt_dve = sem("b_pt_ps"), sem("b_pt_act"), sem("b_pt_dve")
        av_ps, ctx_sb, ct_ps, ct_sb, o_ps = (sem("b_" + n) for n in ("av_ps", "ctx_sb", "ct_ps", "ct_sb", "o_ps"))
        bias_in, yin_sb = sem("bias_in"), sem("yin_sb")
        st2, mv2_s, var2_s, rstd2_s, yh_sb = (sem("b_" + n) for n in ("st2", "mv2", "var2", "rstd2", "yh"))
        tt_ps, tok_sb, thi_sb, tlo_sb = (sem("b_" + n) for n in ("tt_ps", "tok", "thi", "tlo"))
        gap_sb = sem("gap_sb")
        lo_sb = [sem("lo_dve"), sem("lo_pool")]
        y_half = sem("y_half")
        g_ps, route, route_e, route_p = sem("g_ps"), sem("route"), sem("route_e"), sem("route_p")
        cmb_ps, cmb_sb = sem("cmb_ps"), sem("cmb_sb")
        cb_ps, cb_sb = sem("cb_ps"), sem("cb_sb")
        h_rdy, h_sb, y_rdy, term_sb, acc_sb = (sem("b_" + n) for n in ("h_ps", "h_sb", "y_ps", "term", "acc"))
        z_sb, z_ps = sem("z_sb"), sem("z_ps")
        st3, mv3_s, var3_s, rstd3_s, oh_sb, om_sb, of_sb = (
            sem("b_" + n) for n in ("st3", "mv3", "var3", "rstd3", "oh", "om", "of"))
        x1b_sb = sem("x1b_sb")
        sent = sem("sent")

        q_chunks = dram_q.rearrange("s p (c t) -> c p s t", t=CT)
        res_c = dram_res.rearrange("s (c q j) two d -> c j s q (two d)", q=NQ, j=4)
        out_c = out.rearrange("s (c q j) d -> c j s q d", q=NQ, j=4)
        block = ctx.enter_context(nc.Block())

        def later(g, k):
            return not isinstance(g, int) or g >= k

        @block.sync
        def _(sp):
            def load_q(c, p):
                if later(c, 2):
                    sp.wait_ge(sc_ps, c * 4 - 4)
                sp.dma_start(q_c[:, p], q_chunks[c]).then_inc(ld_q[p], 16)

            def load_res(c, p):
                for j in range(4):
                    sp.dma_start(res[j * S:(j + 1) * S, p, :, :, :].rearrange("s q two d -> s q (two d)"),
                                 res_c[c, j]).then_inc(ld_r[p], 16)

            def store(c, p):
                sp.wait_ge(of_sb, c + 1)
                for j in range(4):
                    sp.dma_start(out_c[c, j], res[j * S:(j + 1) * S, p, :, 0, :]).then_inc(sent, 16)

            for c in range(2):
                load_q(c, c)
                load_res(c, c)
            with sp.Fori(0, (NC - 2) // 2) as i:
                for p in range(2):
                    load_q(i * 2 + (p + 2), p)
                    store(i * 2 + p, p)
                    sp.wait_ge(sent, (i * 2 + (p + 1)) * 64)
                    load_res(i * 2 + (p + 2), p)
            store(NC - 2, 0)
            store(NC - 1, 1)
            sp.wait_ge(sent, 64 * NC)

        @block.scalar
        def _(act):

            def exps(c, groups=range(4)):
                for g in groups:
                    act.wait_ge(sub_sb, c * 4 + g + 1)
                    nc.scalar.activation(ex[:, g, :], ex[:, g, :], ACT.Exp).then_inc(ex_sb, 1)

            def probs(c):
                for g in range(2):
                    act.wait_ge(pt_ps, c * 4 + g + 1)
                    if later(c, 1):
                        act.wait_ge(av_ps, c)
                    nc.scalar.activation(ex_t[:, g, :], ps_s[:, g, :], ACT.Copy).then_inc(pt_act, 1)

            def context(c):
                act.wait_ge(ct_ps, c + 1)
                if later(c, 1):
                    act.wait_ge(o_ps, c)
                nc.scalar.activation(ctx_t[:, :], ps_s[:, 1, :], ACT.Identity, bias=vec[:, V_INB + 2:V_INB + 3]
                                     ).then_inc(ct_sb, 1)

            def tokens(c, p):
                act.wait_ge(tt_ps, c + 1)
                if later(c, 2):
                    act.wait_ge(h_rdy, c * 32 - 32)
                nc.scalar.activation(tok_hi[:, p, :], ps_s[:, 3, :], ACT.Identity, bias=vec[:, V_BE1:V_BE1 + 1],
                                     scale=vec[:, V_G1:V_G1 + 1]).then_inc(thi_sb, 1)

            def route_exp(c):
                act.wait_ge(gap_sb, c + 1)
                nc.scalar.activation(gap_e[:, :], gap[:, :], ACT.Exp).then_inc(route_e, 1)

            def combine(c, p):
                act.wait_ge(cmb_ps, c + 1)
                if later(c, 2):
                    act.wait_ge(cb_ps, c * 8 - 7)
                nc.scalar.activation(comb_t[:, p, :], a_ps[0:3 * E, :].bitcast(BF16)[:, 0:TOK], ACT.Copy
                                     ).then_inc(cmb_sb, 1)

            def weights(c, e):
                act.wait_ge(cb_ps, c * 8 + e + 1)
                if later(c, 1) or e >= 2:
                    act.wait_ge(term_sb, c * 8 + e - 1)
                nc.scalar.activation(comb_b[:, e % 2, :], a_ps[:, :], ACT.Copy).then_inc(cb_sb, 1)

            def relus(c, e, half):
                for f in (2 * half, 2 * half + 1):
                    act.wait_ge(h_rdy, c * 32 + e * 4 + f + 1)
                    if later(c, 1) or e >= 2:
                        act.wait_ge(y_rdy, c * 8 + e - 1)
                    if later(c, 1) or e:
                        act.wait_ge(lo_sb[f % 2], c * E * 2 + e * 2 + half - 1)
                    bias = vec[:, V_B1 + e * FC + f:V_B1 + e * FC + f + 1]
                    nc.scalar.activation(hid_x[:, f, :], h_ps[f % 2][:, :], ACT.Relu, bias=bias)
                    nc.scalar.activation(hid_hi[:, e % 2, f, :], h_ps[f % 2][:, :], ACT.Relu, bias=bias
                                         ).then_inc(h_sb, 1)

            exps(0)
            probs(0)
            context(0)
            tokens(0, 0)
            route_exp(0)

            def step(c, p, first, last):
                for e in range(E):
                    relus(c, e, 0)
                    if e in (2, 3) and not last:
                        exps(c + 1, (0,) if e == 2 else (3,))
                    if e == 6 and not last:
                        tokens(c + 1, 1 - p)
                    if e and e != 3:
                        weights(c, e - 1)
                    elif e == 0 and not first:
                        weights(c - 1, E - 1)
                    relus(c, e, 1)
                    if e == 3:
                        weights(c, e - 1)
                    if e == 0:
                        combine(c, p)
                    if last:
                        continue
                    if e == 2:
                        exps(c + 1, (1, 2))
                    if e == 3:
                        probs(c + 1)
                    if e == 4:
                        context(c + 1)
                    if e == 7:
                        route_exp(c + 1)

            run_steps(act, NC, step)
            weights(NC - 1, E - 1)

        @block.vector
        def _(dve):
            def hold(cell):
                nc.vector.memset(held[:, cell:cell + 1], 0.0)

            def keys(c):
                if later(c, 1):
                    dve.wait_ge(tt_ps, c)
                for h in range(QUAD):
                    nc.vector.tensor_scalar(k_bd[:, :, h, :], k_all[:, bass.ts(c, CT), :], quad_mask[:, h:h + 1], None,
                                            ALU.mult).then_inc(kbd_rdy, 1)

            def repeat_tokens(c):
                if later(c, 1):
                    dve.wait_ge(av_ps, c)
                nc.vector.tensor_copy(s_c[:, :, :, :], src_all[:, bass.ts(c, CT), :].unsqueeze(2).to_broadcast(
                    [P, CT, 4, S])).then_inc(s_rdy, 1)

            def values(c, quarters=range(NQ)):
                mask = row_mask[:, :].unsqueeze(1).unsqueeze(3).to_broadcast([P, 16, QUAD, FD])
                for q in quarters:
                    dve.wait_ge(v_ps, c * 4 + q + 1)
                    if later(c, 1):
                        dve.wait_ge(av_ps, c)
                    nc.vector.tensor_tensor(
                        v_bd[:, q * 4:q * 4 + 4, :, :, :].rearrange("p t g h d -> p (t g) h d"),
                        ps_s[:, q, :].rearrange("p (n h d) -> p n h d", h=QUAD, d=FD), mask, ALU.mult
                    ).then_inc(v_rdy, 1)

            def softmax_in(c, groups=range(4)):
                for g in groups:
                    dve.wait_ge(sc_ps, c * 4 + g + 1)
                    if later(c, 1):
                        dve.wait_ge(sub_sb, c * 4 - 4 + g + 1)
                        dve.wait_ge(pt_ps, c * 4 - 4 + g + 1)
                    v = ps_s[:, g, :].rearrange("p (r s) -> p r s", s=S)
                    nc.vector.tensor_reduce(neg_max[:, g, :], v, AX_X, ALU.max, negate=True).then_inc(mx_sb, 1)
                    dve.wait_ge(mx_sb, c * 4 + g + 1)
                    nc.vector.tensor_tensor(ex[:, g, :].rearrange("p (r s) -> p r s", s=S), v,
                                            neg_max[:, g, :].unsqueeze(2).to_broadcast([P, 16, S]), ALU.add
                                            ).then_inc(sub_sb, 1)

            def sums(c):
                if later(c, 1):
                    dve.wait_ge(rec_sb, c)
                for g in range(4):
                    dve.wait_ge(ex_sb, c * 4 + g + 1)
                    nc.vector.tensor_reduce(row_sum[:, g, :], ex[:, g, :].rearrange("p (r s) -> p r s", s=S),
                                            AX_X, ALU.add).then_inc(sum_sb, 1)
                dve.wait_ge(sum_sb, c * 4 + 4)
                if later(c, 1):
                    dve.wait_ge(ctx_sb, c * 4)
                nc.vector.reciprocal(row_rec[:, :, :], row_sum[:, :, :]).then_inc(rec_sb, 1)

            def probs(c):
                for g in range(2, 4):
                    dve.wait_ge(pt_ps, c * 4 + g + 1)
                    if later(c, 1):
                        dve.wait_ge(av_ps, c)
                    nc.vector.tensor_copy(ex_t[:, g, :], ps_s[:, g, :]).then_inc(pt_dve, 1)

            def context(c):
                dve.wait_ge(av_ps, c + 1)
                dve.wait_ge(rec_sb, c + 1)
                if later(c, 1):
                    dve.wait_ge(ct_ps, c)
                for g in range(4):
                    cols = slice(g * 32, g * 32 + 32)
                    nc.vector.tensor_tensor(
                        ctx_tok[:, :, cols].rearrange("p q (h d) -> p q h d", h=QUAD),
                        ps_s[:, 0, :].rearrange("p (q n) -> p q n", q=NQ)[:, :, cols].rearrange(
                            "p q (h d) -> p q h d", h=QUAD),
                        row_rec[:, g, :].rearrange("p (q h) -> p q h", q=NQ).unsqueeze(3).to_broadcast(
                            [P, NQ, QUAD, FD]), ALU.mult).then_inc(ctx_sb, 1)

            def norm1(c, p):
                dve.wait_ge(o_ps, c + 1)
                dve.wait_ge(bias_in, c + 1)
                y_in = res[:, p, :, 1, :]
                nc.vector.tensor_tensor(y_in, ps_s[:, 2, :].rearrange("p (q d) -> p q d", q=NQ),
                                        res[:, p, :, 1, :], ALU.add).then_inc(yin_sb, 1)
                dve.wait_ge(yin_sb, c + 1)
                if later(c, 1):
                    dve.wait_ge(mv2_s, c * 4)
                    dve.wait_ge(yh_sb, c * 4)
                for q in range(NQ):
                    nc.vector.bn_stats(stats[:, q, :], y_in[:, q, :]).then_inc(st2, 1)
                dve.wait_ge(st2, c * 4 + 4)
                hold(2)
                for q in range(NQ):
                    nc.vector.bn_aggr(mv[:, q, :], stats[:, q, :]).then_inc(mv2_s, 1)
                dve.wait_ge(mv2_s, c * 4 + 4)
                nc.vector.tensor_scalar(var[:, :], mv[:, :, 1], EPS_LN, None, ALU.add).then_inc(var2_s, 1)

            def normed1(c, p):
                y_in = res[:, p, :, 1, :]
                dve.wait_ge(rstd2_s, c + 1)
                if later(c, 1):
                    dve.wait_ge(tt_ps, c)
                for q in range(NQ):
                    nc.vector.tensor_scalar(y_hat[:, q, :], y_in[:, q, :], mv[:, q, 0:1], rstd[:, q:q + 1],
                                            ALU.subtract, ALU.mult).then_inc(yh_sb, 1)

            def tokens(c, p):
                dve.wait_ge(tt_ps, c + 1)
                if later(c, 2):
                    dve.wait_ge(z_sb, c - 1)
                dve.wait_ge(thi_sb, c + 1)
                nc.vector.tensor_scalar(tok_t[:, p, :], ps_s[:, 3, :], vec[:, V_G1:V_G1 + 1], vec[:, V_BE1:V_BE1 + 1],
                                        ALU.mult, ALU.add).then_inc(tok_sb, 1)
                dve.wait_ge(tok_sb, c + 1)
                if later(c, 2):
                    dve.wait_ge(h_rdy, c * 32 - 32)
                nc.vector.tensor_tensor(tok_lo[:, p, :], tok_t[:, p, :], tok_hi[:, p, :].bitcast(F32), ALU.subtract
                                        ).then_inc(tlo_sb, 1)

            def routing(c, start):
                n = [0 if start else 4]

                def link(ins):
                    n[0] += 1
                    ins.then_inc(route, 1)
                    dve.wait_ge(route, c * ROUTE + n[0])

                if start:
                    dve.wait_ge(g_ps, c + 1)
                    link(nc.vector.tensor_tensor(logit[:, :, :], ps_s[:, 0, 0:NQ * E].rearrange("p (q e) -> p q e", q=NQ),
                                                 gate_bias[:, :].unsqueeze(1).to_broadcast([P, NQ, E]), ALU.add))
                    hold(4)
                    for q in range(NQ):
                        ins = nc.vector.max(top[:, q, :], logit[:, q, :])
                    link(ins)
                    nc.vector.tensor_tensor(gap[:, :], top[:, :, 1], top[:, :, 0], ALU.subtract).then_inc(gap_sb, 1)
                    for q in range(NQ):
                        ins = nc.vector.max_index(top_i[:, q, :], top[:, q, :], logit[:, q, :])
                    link(ins)
                    link(nc.vector.tensor_copy(top_f[:, :, :], top_i[:, :, 0:2]))
                    return
                dve.wait_ge(route_e, c + 1)
                link(nc.vector.tensor_scalar(wt_den[:, :], gap_e[:, :], 1.0, None, ALU.add))
                link(nc.vector.reciprocal(wt[:, :, 0], wt_den[:, :]))
                link(nc.vector.tensor_tensor(wt[:, :, 1], wt[:, :, 0], gap_e[:, :], ALU.mult))
                for k in range(2):
                    link(nc.vector.tensor_tensor(pick[:, k, :, :], iota8[:, :, :],
                                                 top_f[:, :, k:k + 1].to_broadcast([P, NQ, E]), ALU.is_equal))
                for k in range(2):
                    link(nc.vector.tensor_tensor(pick[:, k, :, :], pick[:, k, :, :],
                                                 wt[:, :, k:k + 1].to_broadcast([P, NQ, E]), ALU.mult))
                link(nc.vector.tensor_tensor(comb[:, :, :], pick[:, 0, :, :], pick[:, 1, :, :], ALU.add))
                if later(c, 1):
                    dve.wait_ge(cmb_ps, c)
                link(nc.vector.tensor_copy(part_bf[:, :, 0, :], comb[:, :, :]))
                link(nc.vector.tensor_tensor(rest[:, 0, :, :], comb[:, :, :], part_bf[:, :, 0, :], ALU.subtract))
                link(nc.vector.tensor_copy(part_bf[:, :, 1, :], rest[:, 0, :, :]))
                link(nc.vector.tensor_tensor(rest[:, 1, :, :], rest[:, 0, :, :], part_bf[:, :, 1, :], ALU.subtract))
                link(nc.vector.tensor_copy(part_bf[:, :, 2, :], rest[:, 1, :, :]))
                assert n[0] == ROUTE

            def weigh(c, e, p):
                dve.wait_ge(y_rdy, c * E + e + 1)
                dve.wait_ge(cb_sb, c * E + e + 1)
                if e >= 3:
                    dve.wait_ge(acc_sb, c * (E - 1) + e - 2)
                elif e and later(c, 1):
                    dve.wait_ge(acc_sb, c * (E - 1))
                dst = acc[:, p, :] if e == 0 else term[:, e % 2, :]
                nc.vector.scalar_tensor_tensor(dst, y_ps[:, :], vec[:, V_B2 + e:V_B2 + e + 1], comb_b[:, e % 2, :],
                                               ALU.add, ALU.mult).then_inc(term_sb, 1)

            def low_part(c, e, half):
                f = 2 * half
                dve.wait_ge(h_sb, c * E * FC + e * FC + f + 1)
                if later(c, 1) or e:
                    dve.wait_ge(y_rdy if half else y_half, c * E + e)
                nc.vector.tensor_tensor(hid_lo[:, f, :], hid_x[:, f, :], hid_hi[:, e % 2, f, :].bitcast(F32),
                                    ALU.subtract).then_inc(lo_sb[0], 1)

            def finish(c, p):
                dve.wait_ge(z_ps, c + 1)
                z = a_ps[:, :].rearrange("p (q d) -> p q d", q=NQ)
                for q in range(NQ):
                    nc.vector.bn_stats(stats3[:, q, :], z[:, q, :]).then_inc(st3, 1)
                dve.wait_ge(st3, c * NQ + NQ)
                hold(3)
                for q in range(NQ):
                    nc.vector.bn_aggr(mv3[:, q, :], stats3[:, q, :]).then_inc(mv3_s, 1)
                dve.wait_ge(mv3_s, c * NQ + NQ)
                nc.vector.tensor_scalar(var3[:, :], mv3[:, :, 1], EPS_LN, None, ALU.add).then_inc(var3_s, 1)

            def finished(c, p):
                z = a_ps[:, :].rearrange("p (q d) -> p q d", q=NQ)
                dve.wait_ge(rstd3_s, c + 1)
                for q in range(NQ):
                    nc.vector.tensor_scalar(o_hat[:, q, :], z[:, q, :], mv3[:, q, 0:1], rstd3[:, q:q + 1],
                                            ALU.subtract, ALU.mult).then_inc(oh_sb, 1)
                dve.wait_ge(oh_sb, c * NQ + NQ)
                nc.vector.tensor_tensor(o_hat[:, :, :], o_hat[:, :, :], g2[:, :].unsqueeze(1).to_broadcast([P, NQ, D]),
                                        ALU.mult).then_inc(om_sb, 1)
                dve.wait_ge(om_sb, c + 1)
                dve.wait_ge(x1b_sb, c + 1)
                nc.vector.tensor_tensor(res[:, p, :, 0, :], o_hat[:, :, :], res[:, p, :, 0, :], ALU.add
                                        ).then_inc(of_sb, 1)

            repeat_tokens(0)
            keys(0)
            values(0)
            softmax_in(0)
            probs(0)
            sums(0)
            context(0)
            norm1(0, 0)
            normed1(0, 0)
            tokens(0, 0)
            routing(0, True)

            def step(c, p, first, last):
                if not last:
                    repeat_tokens(c + 1)
                low_part(c, 0, 0)
                routing(c, False)
                if not last:
                    keys(c + 1)
                if not first:
                    weigh(c - 1, 7, 1 - p)
                low_part(c, 0, 1)
                if not last:
                    values(c + 1)
                low_part(c, 1, 0)
                weigh(c, 0, p)
                low_part(c, 1, 1)
                if not last:
                    softmax_in(c + 1, (0, 1))
                low_part(c, 2, 0)
                if not last:
                    softmax_in(c + 1, (2, 3))
                weigh(c, 1, p)
                low_part(c, 2, 1)
                if not first:
                    finish(c - 1, 1 - p)
                low_part(c, 3, 0)
                if not first:
                    finished(c - 1, 1 - p)
                weigh(c, 2, p)
                low_part(c, 3, 1)
                if not last:
                    probs(c + 1)
                low_part(c, 4, 0)
                if not last:
                    sums(c + 1)
                    context(c + 1)
                weigh(c, 3, p)
                low_part(c, 4, 1)
                low_part(c, 5, 0)
                if not last:
                    norm1(c + 1, 1 - p)
                weigh(c, 4, p)
                low_part(c, 5, 1)
                if not last:
                    normed1(c + 1, 1 - p)
                low_part(c, 6, 0)
                if not last:
                    tokens(c + 1, 1 - p)
                weigh(c, 5, p)
                low_part(c, 6, 1)
                if not last:
                    routing(c + 1, True)
                low_part(c, 7, 0)
                weigh(c, 6, p)
                low_part(c, 7, 1)

            run_steps(dve, NC, step)
            weigh(NC - 1, E - 1, 1)
            finish(NC - 1, 1)
            finished(NC - 1, 1)

        @block.gpsimd
        def _(pool):
            def biases(c, p):
                pool.wait_ge(ld_r[p], c * 32 + (64 - 32 * p))
                nc.gpsimd.tensor_tensor(res[:, p, :, 1, :], res[:, p, :, 1, :],
                                        out_bias[:, :].unsqueeze(1).to_broadcast([P, NQ, D]), ALU.add
                                        ).then_inc(bias_in, 1)
                nc.gpsimd.tensor_tensor(res[:, p, :, 0, :], res[:, p, :, 0, :],
                                        be2[:, :].unsqueeze(1).to_broadcast([P, NQ, D]), ALU.add).then_inc(x1b_sb, 1)

            def rstd_1(c):
                pool.wait_ge(var2_s, c + 1)
                if later(c, 1):
                    pool.wait_ge(yh_sb, c * NQ)
                nc.gpsimd.tensor_tensor(rstd[:, :], var[:, :], neg_half[:, 0:NQ], ALU.pow).then_inc(rstd2_s, 1)

            def rstd_2(c):
                pool.wait_ge(var3_s, c + 1)
                nc.gpsimd.tensor_tensor(rstd3[:, :], var3[:, :], neg_half[:, 0:NQ], ALU.pow).then_inc(rstd3_s, 1)

            def add(c, e, p):
                pool.wait_ge(term_sb, c * E + e + 1)
                if later(c, 1) or e > 1:
                    pool.wait_ge(acc_sb, c * (E - 1) + e - 1)
                nc.gpsimd.tensor_tensor(acc[:, p, :], acc[:, p, :], term[:, e % 2, :], ALU.add).then_inc(acc_sb, 1)

            def residual(c, p):
                pool.wait_ge(acc_sb, (c + 1) * (E - 1))
                nc.gpsimd.tensor_tensor(acc[:, p, :], acc[:, p, :], tok_t[:, p, :], ALU.add).then_inc(z_sb, 1)

            def low_part(c, e, half):
                f = 2 * half + 1
                pool.wait_ge(h_sb, c * E * FC + e * FC + f + 1)
                if later(c, 1) or e:
                    pool.wait_ge(y_rdy if half else y_half, c * E + e)
                nc.gpsimd.tensor_tensor(hid_lo[:, f, :], hid_x[:, f, :], hid_hi[:, e % 2, f, :].bitcast(F32),
                                    ALU.subtract).then_inc(lo_sb[1], 1)

            biases(0, 0)
            rstd_1(0)

            def step(c, p, first, last):
                for e in range(E):
                    if e == 3 and not first:
                        rstd_2(c - 1)
                    low_part(c, e, 0)
                    if e == 5 and not last:
                        rstd_1(c + 1)
                    low_part(c, e, 1)
                    if e == 0 and not first:
                        add(c - 1, E - 1, 1 - p)
                        residual(c - 1, 1 - p)
                    if e == 4 and not last:
                        biases(c + 1, 1 - p)
                    if e >= 2:
                        add(c, e - 1, p)

            run_steps(pool, NC, step)
            add(NC - 1, E - 1, 1)
            residual(NC - 1, 1)
            rstd_2(NC - 1)

        @block.tensor
        def _(pe):
            def values(c):
                pe.wait_ge(s_rdy, c + 1)
                if later(c, 1):
                    pe.wait_ge(route, c * ROUTE - ROUTE + 1)
                for q in range(NQ):
                    for j in range(4):
                        mm = nc.tensor.matmul(ps_s[:, q, j * P:(j + 1) * P], s_c[:, q * 4 + j, :, :], proj_t[:, 2, :],
                                              start=True, stop=True)
                    mm.then_inc(v_ps, 1)

            def scores_wait(c, p):
                pe.wait_ge(ld_q[p], c * 8 + (16 - 8 * p))
                pe.wait_ge(kbd_rdy, c * QUAD + QUAD)
                pe.wait_ge(v_rdy, c * 4 + 4)

            def scores(c, p, q, groups=range(4)):
                for g in groups:
                    rows = slice(g * 32, g * 32 + 32)
                    for j in range(4):
                        t = q * 4 + j
                        mm = nc.tensor.matmul(ps_s[j * S:(j + 1) * S, g, q * P:(q + 1) * P], q_c[rows, p, :, t],
                                              k_bd[rows, t, :, :], start=True, stop=True)
                    if q == NQ - 1:
                        mm.then_inc(sc_ps, 1)

            def probs(c, groups=range(4)):
                for g in groups:
                    pe.wait_ge(ex_sb, c * 4 + g + 1)
                    for q in range(NQ):
                        mm = nc.tensor.transpose(ps_s[:, g, q * P:(q + 1) * P], ex[:, g, q * P:(q + 1) * P], ident[:, :])
                    mm.then_inc(pt_ps, 1)

            def attend(c):
                pe.wait_ge(pt_act, c * 2 + 2)
                pe.wait_ge(pt_dve, c * 2 + 2)
                for q in range(NQ):
                    for g in range(4):
                        for j in range(4):
                            o = q * P + g * 32
                            mm = nc.tensor.matmul(ps_s[j * S:(j + 1) * S, 0, o:o + 32],
                                                  ex_t[:, g, q * P + j * S:q * P + (j + 1) * S],
                                                  v_bd[:, q * 4 + j, g, :, :], start=True, stop=True)
                mm.then_inc(av_ps, 1)

            def turn(bank, tile, done):
                for q in range(NQ):
                    mm = nc.tensor.transpose(bank[:, q * P:(q + 1) * P], tile[:, q, :], ident[:, :])
                mm.then_inc(done, 1)

            def context(c):
                pe.wait_ge(ctx_sb, c * 4 + 4)
                turn(ps_s[:, 1, :], ctx_tok, ct_ps)

            def out_proj(c):
                pe.wait_ge(ct_sb, c + 1)
                for q in range(NQ):
                    mm = nc.tensor.matmul(ps_s[:, 2, q * D:(q + 1) * D], ctx_t[:, q * P:(q + 1) * P], proj_t[:, 3, :],
                                          start=True, stop=True)
                mm.then_inc(o_ps, 1)

            def tokens(c):
                pe.wait_ge(yh_sb, c * NQ + NQ)
                turn(ps_s[:, 3, :], y_hat, tt_ps)

            def gate(c, p):
                pe.wait_ge(tok_sb, c + 1)
                for q in range(NQ):
                    mm = nc.tensor.matmul(ps_s[:, 0, q * E:(q + 1) * E], tok_t[:, p, q * P:(q + 1) * P],
                                          vec[:, V_GATE:V_GATE + E], start=True, stop=True)
                mm.then_inc(g_ps, 1)

            def combine(c):
                pe.wait_ge(route, c * ROUTE + ROUTE)
                if later(c, 1):
                    pe.wait_ge(cb_sb, c * E)
                dst = a_ps[0:3 * E, :].bitcast(BF16)
                for q in range(NQ):
                    mm = nc.tensor.transpose(dst[:, q * P:(q + 1) * P],
                                             part_bf[:, q, :, :].rearrange("p k e -> p (k e)"), ident_bf[:, :])
                mm.then_inc(cmb_ps, 1)

            def weights(c, e, p):
                if e == 0:
                    pe.wait_ge(cmb_sb, c + 1)
                else:
                    pe.wait_ge(cb_sb, c * E + e)
                if e == 2 and later(c, 1):
                    pe.wait_ge(oh_sb, c * NQ)
                nc.tensor.matmul(a_ps[:, :], sel_bf[:, e, :], comb_t[:, p, :], start=True, stop=True).then_inc(cb_ps, 1)

            def hidden(c, e, p, half):
                if e == 0 and half == 0:
                    pe.wait_ge(thi_sb, c + 1)
                    pe.wait_ge(tlo_sb, c + 1)
                for f in (2 * half, 2 * half + 1):
                    n = e * FC + f
                    if later(c, 1) or n >= 2:
                        pe.wait_ge(h_sb, c * E * FC + n - 1)
                    cols = slice(n * P, (n + 1) * P)
                    dst = h_ps[f % 2][:, :]
                    nc.tensor.matmul(dst, w1_hi[:, cols], tok_hi[:, p, :], start=True, stop=False)
                    nc.tensor.matmul(dst, w1_hi[:, cols], tok_lo[:, p, :], start=False, stop=False)
                    nc.tensor.matmul(dst, w1_lo[:, cols], tok_hi[:, p, :], start=False, stop=True).then_inc(h_rdy, 1)

            def expert_out(c, e, half, before_last=None):
                if half == 0 and (later(c, 1) or e):
                    pe.wait_ge(term_sb, c * E + e)
                fs = (2 * half, 2 * half + 1)
                for f in fs:
                    pe.wait_ge(h_sb, c * E * FC + e * FC + f + 1)
                    hi = hid_hi[:, e % 2, f, :]
                    nc.tensor.matmul(y_ps[:, :], w2_hi[:, e, f, :], hi, start=(f == 0), stop=False)
                    nc.tensor.matmul(y_ps[:, :], w2_lo[:, e, f, :], hi, start=False, stop=False)
                for f in fs:
                    pe.wait_ge(lo_sb[f % 2], c * E * 2 + e * 2 + half + 1)
                    if f % 2 and before_last:
                        before_last()
                    mm = nc.tensor.matmul(y_ps[:, :], w2_hi[:, e, f, :], hid_lo[:, f, :],
                                          start=False, stop=(f == FC - 1))
                mm.then_inc(y_rdy if half else y_half, 1)

            def sums(c, p):
                pe.wait_ge(z_sb, c + 1)
                pe.wait_ge(cb_sb, c * E + E + 2)
                for q in range(NQ):
                    mm = nc.tensor.transpose(a_ps[:, q * P:(q + 1) * P], acc[:, p, q * P:(q + 1) * P], ident[:, :])
                mm.then_inc(z_ps, 1)

            values(0)
            scores_wait(0, 0)
            for g in range(4):
                for q in range(NQ):
                    scores(0, 0, q, (g,))
            probs(0)
            attend(0)
            context(0)
            out_proj(0)
            tokens(0)
            gate(0, 0)

            def step(c, p, first, last):
                ahead = {
                    (0, 3): lambda: values(c + 1),
                    (1, 1): lambda: scores(c + 1, 1 - p, 0), (1, 2): lambda: scores(c + 1, 1 - p, 1),
                    (1, 3): lambda: scores(c + 1, 1 - p, 2), (2, 0): lambda: scores(c + 1, 1 - p, 3),
                    (3, 0): lambda: probs(c + 1, (0, 1)), (3, 2): lambda: probs(c + 1, (2, 3)),
                    (4, 2): lambda: attend(c + 1), (4, 3): lambda: context(c + 1), (5, 1): lambda: out_proj(c + 1),
                    (6, 1): lambda: tokens(c + 1), (7, 0): lambda: gate(c + 1, 1 - p)}

                def next_chunk(e, place):
                    if (e, place) in ahead and not last:
                        ahead[e, place]()

                for e in range(E):
                    before = (c, e - 1, p) if e else (c - 1, E - 1, 1 - p)
                    hidden(c, e, p, 0)
                    if e == 3 and not first:
                        sums(c - 1, 1 - p)
                    next_chunk(e, 0)
                    if e or not first:
                        expert_out(before[0], before[1], 0,
                                   (lambda: scores_wait(c + 1, 1 - p)) if e == 1 and not last else None)
                    next_chunk(e, 1)
                    if e not in (0, 3) or (e == 0 and not first):
                        weights(*before)
                    hidden(c, e, p, 1)
                    next_chunk(e, 2)
                    if e == 3:
                        weights(*before)
                    if e or not first:
                        expert_out(before[0], before[1], 1)
                    next_chunk(e, 3)
                    if e == 0:
                        combine(c)

            run_steps(pe, NC, step)
            expert_out(NC - 1, E - 1, 0)
            weights(NC - 1, E - 1, (NC - 1) % 2)
            expert_out(NC - 1, E - 1, 1)
            pe.wait_ge(z_sb, NC)
            pe.wait_ge(cb_sb, NC * E)
            for q in range(NQ):
                mm = nc.tensor.transpose(a_ps[:, q * P:(q + 1) * P], acc[:, 1, q * P:(q + 1) * P], ident[:, :])
            mm.then_inc(z_ps, 1)


_NAMES = {
    "x": "x", "ctx": "ctx_1024", "mask": "mask_BxS2_bk0", "rms": "L0_xattn_rms_scale", "q_w": "L0_xattn_q_w",
    "kv_w": "L0_xattn_kv_w", "wo_x": "L0_xattn_out_w", "in_w": "L0_ffn_in_proj_w", "in_b": "L0_ffn_in_proj_b",
    "out_w": "L0_ffn_out_w", "out_b": "L0_ffn_out_b", "gate_w": "L0_ffn_gate_w", "gate_b": "L0_ffn_gate_b",
    "w1": "L0_ffn_w1", "b1": "L0_ffn_b1", "w2": "L0_ffn_w2", "b2": "L0_ffn_b2", "ln1_g": "L0_ffn_ln1_g",
    "ln1_b": "L0_ffn_ln1_b", "ln2_g": "L0_ffn_ln2_g", "ln2_b": "L0_ffn_ln2_b",
}


def constants():
    half = HD // 2
    scale = np.float32(10000.0) ** (np.float32(2.0 / HD) * np.arange(half, dtype=np.float32))
    rope = np.zeros((4, P, T), np.float32)
    for n, first in ((0, T), (2, 0)):
        angle = (np.arange(first, first + T, dtype=np.float32)[:, None] / scale).T
        cos, sin = np.cos(angle), np.sin(angle)
        rope[n] = np.tile(np.concatenate([cos, cos]), (NH, 1))
        rope[n + 1] = np.tile(np.concatenate([-sin, sin]), (NH, 1))
    p = np.arange(P)
    sel = np.zeros((3 * E, E, P), np.float32)
    for r in range(3 * E):
        sel[r, r % E] = 1.0
    return {
        "ident": np.eye(P, dtype=np.float32), "rope": rope,
        "quad_mask": ((p % 32)[:, None] // FD == np.arange(QUAD)).astype(np.float32),
        "row_mask": (p[:, None] // 32 == np.arange(QUAD)).astype(np.float32),
        "expert_sel": sel,
        "iota8": np.broadcast_to(np.arange(E, dtype=np.float32), (P, NQ, E)).copy(),
    }


def kernel(**inputs):
    import concourse.bacc as bacc
    from concourse.bass_utils import run_bass_kernel_spmd

    nc = bacc.Bacc("TRN2", target_bir_lowering=False, num_devices=1)
    arrays, args = {}, {}
    given = {short: np.ascontiguousarray(inputs[name]) for short, name in _NAMES.items()}
    for name, array in {**given, **constants()}.items():
        arrays[f"in_{name}"] = array
        args[name] = nc.dram_tensor(f"in_{name}", array.shape, mybir.dt.from_np(array.dtype), kind="ExternalInput").ap()
    out = nc.dram_tensor("out_x", [S, T, D], F32, kind="ExternalOutput").ap()
    build(nc, args, out)
    r = run_bass_kernel_spmd(nc, [arrays], core_ids=[0])
    return r.results[0]["out_x"]
```
